# Optimizing a Trainium2 kernel written in Bass

```python
import numpy as np
import jax
import jax.numpy as jnp

def _softmax(x, axis=-1):
    return jax.nn.softmax(x, axis=axis)
def _gelu(x):
    return jax.nn.gelu(x, approximate=True)
def _silu(x):
    return jax.nn.silu(x)
def _sigmoid(x):
    return jax.nn.sigmoid(x)
def _layernorm(x, axis=-1, eps=1e-5):
    m = jnp.mean(x, axis=axis, keepdims=True)
    v = jnp.var(x, axis=axis, keepdims=True)
    return (x - m) / jnp.sqrt(v + eps)
def _scatter_add(tgt, idx, src, axis=0):
    return tgt.at[idx].add(src)
def _segment_sum(src, seg, n):
    return jax.ops.segment_sum(src, seg, n)

kernel_name = 'mk_conv_seq_d1_conv_nchw512_2362bf'

def setup_inputs(seed: int = 0):
    np.random.seed(seed)
    _w = jnp.asarray
    def _rec_inputs():
        import jax
        import jax.numpy as jnp
        _gk = jax.random.key(seed)
        x = 7.22e-05 + 1 * jax.random.normal(jax.random.fold_in(_gk, 1), (16, 512, 32, 32), jnp.float32)
        return x
    x = _rec_inputs()
    def _L0_conv_setup():
        import jax, jax.numpy as jnp
        import numpy as np
        N_HEADS = 8
        N_GROUPS = 32
        EPS = 1e-05
        key = jax.random.key(seed)
        ks = jax.random.split(key, 3)
        B, C, H, W = (16, 512, 32, 32)
        x = jax.random.normal(ks[0], (B, C, H, W), dtype=jnp.float32)
        gn_w = jnp.ones((C,), dtype=jnp.float32)
        gn_b = jnp.zeros((C,), dtype=jnp.float32)
        qkv_w = jax.random.normal(ks[1], (3 * C, C), dtype=jnp.float32) * (1.0 / np.sqrt(C))
        qkv_b = jnp.zeros((3 * C,), dtype=jnp.float32)
        proj_w = jax.random.normal(ks[2], (C, C), dtype=jnp.float32) * (1.0 / np.sqrt(C))
        proj_b = jnp.zeros((C,), dtype=jnp.float32)
        return {'x': x, 'gn_w': gn_w, 'gn_b': gn_b, 'qkv_w': qkv_w, 'qkv_b': qkv_b, 'proj_w': proj_w, 'proj_b': proj_b}
    _L0_conv_all = _L0_conv_setup()
    _L0_conv_in = {k: v for k, v in _L0_conv_all.items() if k in ('gn_w', 'gn_b', 'qkv_w', 'qkv_b', 'proj_w', 'proj_b', )}
    del _L0_conv_all

    return {
        "x": x,
        "L0_conv_gn_w": _L0_conv_in["gn_w"],
        "L0_conv_gn_b": _L0_conv_in["gn_b"],
        "L0_conv_qkv_w": _L0_conv_in["qkv_w"],
        "L0_conv_qkv_b": _L0_conv_in["qkv_b"],
        "L0_conv_proj_w": _L0_conv_in["proj_w"],
        "L0_conv_proj_b": _L0_conv_in["proj_b"],
    }

def reference(x, L0_conv_gn_w, L0_conv_gn_b, L0_conv_qkv_w, L0_conv_qkv_b, L0_conv_proj_w, L0_conv_proj_b):
    import jax
    import jax.numpy as jnp
    def _L0_conv_ref(x, gn_w, gn_b, qkv_w, qkv_b, proj_w, proj_b):
        import jax, jax.numpy as jnp
        import numpy as np
        N_HEADS = 8
        N_GROUPS = 32
        EPS = 1e-05
        b, c, h, w = x.shape
        t = h * w
        xf = x.reshape(b, c, t)
        xg = xf.reshape(b, N_GROUPS, -1)
        mean = xg.mean(axis=-1, keepdims=True)
        var = xg.var(axis=-1, keepdims=True)
        xn = ((xg - mean) * jax.lax.rsqrt(var + EPS)).reshape(b, c, t)
        xn = xn * gn_w[:, None] + gn_b[:, None]
        qkv = jnp.einsum('oc,bct->bot', qkv_w, xn) + qkv_b[:, None]
        qkv = qkv.reshape(b * N_HEADS, 3 * c // N_HEADS, t)
        ch = qkv.shape[1] // 3
        q, k, v = jnp.split(qkv, 3, axis=1)
        scale = 1.0 / np.sqrt(np.sqrt(ch))
        weight = jnp.einsum('bct,bcs->bts', q * scale, k * scale)
        weight = jax.nn.softmax(weight.astype(jnp.float32), axis=-1).astype(weight.dtype)
        a = jnp.einsum('bts,bcs->bct', weight, v)
        hh = a.reshape(b, c, t)
        hh = jnp.einsum('oc,bct->bot', proj_w, hh) + proj_b[:, None]
        return (xf + hh).reshape(b, c, h, w)

    def _gn(v, G=32, eps=1e-5):
        B_, C_, H_, W_ = v.shape
        g = v.reshape(B_, G, C_ // G, H_, W_)
        m = jnp.mean(g, axis=(2, 3, 4), keepdims=True)
        s = jnp.var(g, axis=(2, 3, 4), keepdims=True)
        return ((g - m) / jnp.sqrt(s + eps)).reshape(v.shape)

    def _ln_c(v, eps=1e-6):
        m = jnp.mean(v, axis=1, keepdims=True)
        s = jnp.var(v, axis=1, keepdims=True)
        return (v - m) / jnp.sqrt(s + eps)

    def _ln_t(v, eps=1e-5):
        m = jnp.mean(v, axis=-1, keepdims=True)
        s = jnp.var(v, axis=-1, keepdims=True)
        return (v - m) / jnp.sqrt(s + eps)

    def _to_tokens(v):
        B_, C_, H_, W_ = v.shape
        return v.reshape(B_, C_, H_ * W_).transpose(0, 2, 1)
    def _from_tokens(t, like):
        B_, C_, H_, W_ = like.shape
        return t.transpose(0, 2, 1).reshape(B_, C_, H_, W_)

    x = _L0_conv_ref(x, L0_conv_gn_w, L0_conv_gn_b, L0_conv_qkv_w, L0_conv_qkv_b, L0_conv_proj_w, L0_conv_proj_b)
    return x


_drawn_inputs = setup_inputs


def setup_inputs(seed=0):
    import zlib

    import numpy as np

    out = dict(_drawn_inputs(seed))
    spreads = {'L0_conv_gn_w': (1.0, 0.6),
     'L0_conv_gn_b': (0.0, 0.1),
     'L0_conv_qkv_b': (0.0, 0.1),
     'L0_conv_proj_b': (0.0, 0.1)}
    factors = {}
    for name, (base, spread) in spreads.items():
        noise = np.random.default_rng([zlib.crc32(name.encode()), seed]).standard_normal(out[name].shape)
        drawn = base * np.exp(spread * noise) if base else spread * noise
        out[name] = jnp.asarray(drawn.astype(out[name].dtype))
    for name, factor in factors.items():
        out[name] = (out[name] * factor).astype(out[name].dtype)
    return out
```

```python
from contextlib import ExitStack

import concourse.bass as bass
from concourse import mybir

F32 = mybir.dt.float32
F16 = mybir.dt.float16
U32 = mybir.dt.uint32
ALU = mybir.AluOpType
ACT = mybir.ActivationFunctionType
AX = mybir.AxisListType
RMAX = bass.bass_isa.ReduceOp.max

P = 128
HEADS = 8
GROUPS = 32
EPS = 1e-5
HI, LO = 0, 1

XS = 2.0 ** 7
ROW = 2.0 ** 14
TOP = 2.0 ** 15
PS = 2.0 ** 14
RS = 2.0 ** 14

SLOTS = ([("proj", n, m) for n in range(2) for m in range(4)]
         + [("qk", 2, n) for n in range(4)] + [("qk", 3, n) for n in range(4)]
         + [("v", s, 0) for s in range(8)]
         + [("qk", 0, n) for n in range(4)] + [("qk", 1, n) for n in range(4)])
AHEAD = 16
HEAD_START = SLOTS[AHEAD:]
STACK = [0, 1, 0, 2]

STAT_STEP = [1, 18]
MEAN_STEP = [5, 21]
VAR_STEP = [7, 23]
NORM_STEP = [11, 26]


def filler_number(b, slot):
    return b * 32 + 8 + slot


def bass_groupnorm_attention_kernel(nc, x, gn_w, gn_b, qkv_w, qkv_b, proj_w, proj_b, out):
    B, C, HH, WW = x.shape
    T = HH * WW
    D = C // HEADS
    KC = C // P
    PAIRS = HEADS // 2
    ST = T // P
    STEPS = HEADS * ST
    TG = 2 * P
    CPG = C // GROUPS
    assert (C, T, D, KC, STEPS, CPG) == (512, 1024, 64, 4, 64, 16) and B % 2 == 0
    assert CPG * T == 2 ** 14

    xr_v = x.rearrange("b c h w -> b c (h w)")
    out_v = out.rearrange("b c h w -> b c (h w)")

    with ExitStack() as ctx:
        def sb(name, shape, dt):
            return ctx.enter_context(nc.sbuf_tensor(name, shape, dt))

        def sem(name):
            return ctx.enter_context(nc.semaphore(name))

        Wqkv = sb("Wqkv", [P, 2, KC, 3 * C], F16)
        Wp = sb("Wp", [P, 2, KC, C], F16)
        XN = sb("XN", [P, 2, 2, KC, T], F16)
        xc = sb("xc", [P, 2, T], F32)
        V = sb("V", [P, 2, 2, ST, C], F16)
        PT = sb("PT", [P, 2, 2, 2, ST, TG], F16)
        Pr = sb("Pr", [P, T], F32)
        yf = sb("yf", [P, 512], F32)
        nat = sb("nat", [P, 2, 2, 512], F16)
        QS = sb("QS", [P, 3, 2, T], F16)
        KH = sb("KH", [P, 3, 2, T], F16)
        KL = sb("KL", [P, 3, 2, T], F16)
        AT = sb("AT", [P, 2, KC, T], F16)
        rsb = sb("rsb", [P, TG], F32)
        at = sb("at", [P, TG], F32)
        xres = sb("xres", [P, 2, 512], F32)
        id32 = sb("id32", [P, P], F32)
        id16 = sb("id16", [P, P], F16)
        gavg = sb("gavg", [P, P], F32)
        rb = sb("rb", [P, 2, 4, D], F16)
        acc = sb("acc", [P, 2, 4], F32)
        rinv = sb("rinv", [P, 2, 4], F32)
        rscl = sb("rscl", [P, 4], F32)
        nmax = sb("nmax", [P, 4], F32)
        nbias = sb("nbias", [P, 4], F32)
        sscale = sb("sscale", [P, 1], F32)
        cq = sb("cq", [P, 12], F32)
        bq = sb("bq", [P, 12], F32)
        cp = sb("cp", [P, 4], F32)
        bp = sb("bp", [P, 4], F32)
        st6 = sb("st6", [P, 2, 2, 6], F32)
        mv = sb("mv", [P, 2, 2], F32)
        gm = sb("gm", [P, 2], F32)
        dd = sb("dd", [P, 2], F32)
        ex = sb("ex", [P, 2], F32)
        rs = sb("rs", [P, 2], F32)
        hv = sb("hv", [P, 2], F32)
        ny = sb("ny", [P, 2], F32)
        na = sb("na", [P, 2], F32)
        bound = sb("bound", [P, 12], F32)
        tmp = sb("tmp", [P, 12], F32)
        omega = sb("omega", [P, 12], F32)
        top2 = sb("top2", [P, 2], F32)
        gtop = sb("gtop", [P, 2], F32)

        borrowed = PT[:].rearrange("p a b c d e -> p (a b c d e)").bitcast(F32)
        wn = borrowed[:, 0:12 * C].rearrange("p (m c) -> p m c", c=C)
        wpn = borrowed[:, 12 * C:16 * C].rearrange("p (m c) -> p m c", c=C)
        borrowed_v = V[:].rearrange("p a b c d -> p (a b c d)").bitcast(F32)
        prod = borrowed_v[:, 0:12 * C].rearrange("p (m c) -> p m c", c=C)
        gw = borrowed_v[:, 12 * C:13 * C]
        gb = borrowed_v[:, 13 * C:14 * C]
        diag = borrowed_v[:, 14 * C:15 * C].rearrange("p (m c) -> p m c", c=P)
        ones = borrowed_v[:, 15 * C:15 * C + P]

        SC = ctx.enter_context(nc.psum_tensor("SC", [P, 2, T], F32))
        TP = ctx.enter_context(nc.psum_tensor("TP", [P, ST, P], F32))
        AV = ctx.enter_context(nc.psum_tensor("AV", [P, 2, TG], F32))
        FB = ctx.enter_context(nc.psum_tensor("FB", [P, 512], F32))
        wbank = SC[:].rearrange("p a (b m c) -> p (a b) m c", b=2, c=P)

        w_loaded = sem("w_loaded")
        consts = sem("consts")
        setup_pool = sem("setup_pool")
        setup_dve = sem("setup_dve")
        setup_pe = sem("setup_pe")
        w_hi = sem("w_hi")
        w_lo = sem("w_lo")
        xc_loaded = [sem(f"xc_loaded{c}") for c in range(2)]
        res_loaded = [sem(f"res_loaded{c}") for c in range(2)]
        stored = [sem(f"stored{c}") for c in range(2)]
        stacked = [sem(f"stacked{c}") for c in range(2)]
        stat_in = sem("stat_in")
        stat_out = sem("stat_out")
        stat_read = sem("stat_read")
        norm_ready = sem("norm_ready")
        xn_done = sem("xn_done")
        s_done = sem("s_done")
        nb_done = sem("nb_done")
        e_done = sem("e_done")
        t_done = sem("t_done")
        ph_done = sem("ph_done")
        pl_done = sem("pl_done")
        ri_done = sem("ri_done")
        rb_done = sem("rb_done")
        av_done = sem("av_done")
        r_copied = sem("r_copied")
        av_read = sem("av_read")
        at_done = sem("at_done")
        filler_psum = sem("filler_psum")
        y_done = sem("y_done")
        filler_out = sem("filler_out")
        dve_chain = sem("dve_chain")
        pool_chain = sem("pool_chain")

        block = ctx.enter_context(nc.Block())

        def wait(eng, s, value):
            if not isinstance(value, int) or value > 0:
                eng.wait_ge(s, value)

        def apart(eng, *values):
            for value in values:
                if not isinstance(value, int):
                    eng.compute_val(value)
            eng.wait_ge(consts, 3)

        class Chain:

            def __init__(self, eng, s):
                self.eng, self.sem, self.base, self.n, self.alone = eng, s, 0, 0, False

            def __call__(self, ins):
                self.n += 1
                ins.then_inc(self.sem, 1)
                if self.alone:
                    apart(self.eng, self.base + self.n)
                self.eng.wait_ge(self.sem, self.base + self.n)

        def run_batches(eng, batch, chain=None):
            batch(0, 0, True, False)
            if chain:
                before = chain.n
            with eng.Fori(0, B // 2 - 1) as j:
                if chain:
                    chain.base, chain.n = before + j * (2 * chain.per_batch), 0
                batch(j * 2 + 1, 1, False, False)
                batch(j * 2 + 2, 0, False, False)
                if chain:
                    assert chain.n == 2 * chain.per_batch, (chain.n, chain.per_batch)
            if chain:
                chain.base, chain.n = 0, before + (B - 2) * chain.per_batch
            batch(B - 1, 1, False, True)

        def slots_of(b, first, last):
            found = {}
            for s, item in enumerate(SLOTS):
                if first and s < 8 or last and s >= AHEAD:
                    continue
                found[s] = (item, -1 if item[0] == "proj" else 1 if s >= AHEAD else 0)
            return found

        @block.sync
        def _(sp):
            for a in range(2):
                for kind in range(3):
                    src = qkv_w.rearrange("(q a k r) c -> a k r q c", a=2, k=3, r=D)[a, kind]
                    sp.dma_start(wn[a * D:(a + 1) * D, kind * 4:kind * 4 + 4, :], src).then_inc(w_loaded, 16)
                    bsrc = qkv_b.rearrange("(q a k r) -> a k r q", a=2, k=3, r=D)[a, kind]
                    sp.dma_start(bq[a * D:(a + 1) * D, kind * 4:kind * 4 + 4], bsrc,
                                 allow_slow_non_contiguous=True).then_inc(w_loaded, 16)
            sp.dma_start(wpn, proj_w.rearrange("(m p) c -> p m c", p=P)).then_inc(w_loaded, 16)
            sp.dma_start(bp[:], proj_b.rearrange("(m p) -> p m", p=P), allow_slow_non_contiguous=True).then_inc(w_loaded, 16)
            sp.dma_start(gw, gn_w.partition_broadcast(P)).then_inc(w_loaded, 16)
            sp.dma_start(gb, gn_b.partition_broadcast(P)).then_inc(w_loaded, 16)

            def load_chunks(X, r):
                for c in range(2):
                    apart(sp, X * 4 + (2 * r + c - 1))
                    wait(sp, xn_done, X * 4 + (2 * r + c - 1))
                    kc = 2 * r + c
                    sp.dma_start(xc[:, c, :], xr_v[X, kc * P:(kc + 1) * P, :]).then_inc(xc_loaded[c], 16)

            def load_residual(b, i):
                n, m = i // 4, i % 4
                sp.dma_start(xres[:, i % 2, :], xr_v[b, m * P:(m + 1) * P, n * 512:(n + 1) * 512]) \
                    .then_inc(res_loaded[i % 2], 16)

            def store(b, i, F):
                n, m = i // 4, i % 4
                apart(sp, F + 1)
                sp.wait_ge(filler_out, F + 1)
                sp.dma_start(out_v[b, m * P:(m + 1) * P, n * 512:(n + 1) * 512], xres[:, i % 2, :]) \
                    .then_inc(stored[i % 2], 16)
                apart(sp, b * 64 + 16 * (i // 2 + 1))
                sp.wait_ge(stored[i % 2], b * 64 + 16 * (i // 2 + 1))

            def stack_qk(b, pair, n, F):
                kind, half = n // 2, n % 2
                cols = slice(half * 512, half * 512 + 512)
                buf = STACK[pair]
                scored = b * STEPS + [-16, -32, 16, 0][pair]
                apart(sp, F + 1, scored)
                sp.wait_ge(filler_out, F + 1)
                wait(sp, s_done, scored)
                for a in range(2):
                    rows = slice(a * D, a * D + D)
                    if kind == 0:
                        for part in (HI, LO):
                            sp.dma_start(QS[part * D:part * D + D, buf, a, cols], nat[rows, half, part, :]) \
                                .then_inc(stacked[half], 16)
                    else:
                        for part, dst in ((HI, KH), (LO, KL)):
                            for z in range(2):
                                sp.dma_start(dst[z * D:z * D + D, buf, a, cols], nat[rows, half, part, :]) \
                                    .then_inc(stacked[half], 16)

            load_chunks(0, 0)
            load_chunks(0, 1)
            for i in range(2):
                load_residual(0, i)
            for F, item in enumerate(HEAD_START):
                if item[0] == "qk":
                    stack_qk(0, item[1], item[2], F)

            def batch(b, par, first, last):
                if not last:
                    load_chunks(b + 1, 0)
                for s, (item, off) in slots_of(b, first, last).items():
                    F = filler_number(b, s)
                    if s == 8 and not last:
                        load_chunks(b + 1, 1)
                    if item[0] == "proj":
                        store(b - 1, s, F)
                        load_residual(b - 1 if s < 6 else b, (s + 2) % 8)
                    if item[0] == "qk":
                        stack_qk(b + off, item[1], item[2], F)

            run_batches(sp, batch)
            for s in range(8):
                store(B - 1, s, filler_number(B - 1, AHEAD + s))
                if s < 6:
                    load_residual(B - 1, s + 2)

        @block.tensor
        def _(pe):
            pe.wait_ge(consts, 3)
            pe.wait_ge(setup_dve, 1)
            nc.tensor.matmul(AV[:].rearrange("p a t -> p (a t)"), ones, diag.rearrange("p m c -> p (m c)"),
                             start=True, stop=True).then_inc(setup_pe, 1)
            for m in range(16):
                if m >= 4:
                    pe.wait_ge(w_lo, m - 3)
                if m == 0:
                    pe.wait_ge(setup_dve, 2)
                if m == 12:
                    pe.wait_ge(setup_dve, 3)
                src = wn[:, m, :] if m < 12 else wpn[:, m - 12, :]
                for kc in range(KC):
                    last = nc.tensor.transpose(wbank[:, m % 4, kc, :], src[:, kc * P:(kc + 1) * P], id32[:])
                last.then_inc(setup_pe, 1)

            def filler(F, item, b, par, part_of):
                kind, i0, i1 = item
                if part_of == 0:
                    wait(pe, y_done, F)
                    if kind == "v" and i0 == 0:
                        pe.wait_ge(xn_done, b * 4 + 4)
                    if kind == "proj" and i1 == 0:
                        pe.wait_ge(at_done, b * 16 + (14 if i0 == 0 else 16))
                for kc in (0, 1) if part_of == 0 else (2, 3):
                    for ps, pm in ((HI, HI), (HI, LO), (LO, HI)):
                        if kind == "qk":
                            m = (i1 // 2) * 4 + i0
                            lhsT = Wqkv[:, ps, kc, m * P:(m + 1) * P]
                            rhs = XN[:, par, pm, kc, (i1 % 2) * 512:(i1 % 2) * 512 + 512]
                        elif kind == "v":
                            lhsT = XN[:, par, ps, kc, i0 * P:(i0 + 1) * P]
                            rhs = Wqkv[:, pm, kc, 2 * C:3 * C]
                        else:
                            lhsT = Wp[:, ps, kc, i1 * P:(i1 + 1) * P]
                            rhs = AT[:, pm, kc, i0 * 512:i0 * 512 + 512]
                        last = nc.tensor.matmul(FB[:], lhsT, rhs, start=(kc == 0 and ps == pm),
                                                stop=(kc == 3 and ps == LO))
                if part_of == 1:
                    last.then_inc(filler_psum, 1)

            def group_average(count, fillers_before):
                wait(pe, y_done, fillers_before)
                pe.wait_ge(stat_in, count)
                src = mv[:, :, 0] if count_stage[0] == 0 else ex[:]
                nc.tensor.matmul(FB[:, 0:2], gavg[:], src, start=True, stop=True).then_inc(stat_out, 1)

            count_stage = [0]

            def scores(b, i, first_tile):
                pair, u, j, a = i // 16, (i // 4) % 4, (i % 4) // 2, i % 2
                t0 = (2 * u + j) * P
                if i % 16 == 0:
                    for half in range(2):
                        pe.wait_ge(stacked[half], b * (192 * PAIRS) + 192 * (pair + 1))
                if not (first_tile and i < 2):
                    pe.wait_ge(e_done, b * STEPS + (i - 1))
                for half in range(2):
                    for K, start in ((KH, True), (KL, False)):
                        last = nc.tensor.matmul(SC[:, i % 2, half * 512:half * 512 + 512],
                                                QS[:, STACK[pair], a, t0:t0 + P],
                                                K[:, STACK[pair], a, half * 512:half * 512 + 512],
                                                start=start, stop=not start)
                last.then_inc(s_done, 1)

            def transposes(b, i):
                pe.wait_ge(e_done, b * STEPS + (i + 1))
                wait(pe, pl_done, b * STEPS + i)
                for c in range(ST):
                    last = nc.tensor.transpose(TP[:, c, :], Pr[:, c * P:(c + 1) * P], id32[:])
                last.then_inc(t_done, 1)

            def weighted_sum(b, g, k, par):
                pair = g // 4
                if k == 0:
                    pe.wait_ge(pl_done, b * STEPS + 4 * (g + 1))
                    wait(pe, av_read, b * 16 + g)
                    if g == 0:
                        pe.wait_ge(filler_out, 8 if isinstance(b, int) and b == 0 else b * 32)
                for c in (2 * k, 2 * k + 1):
                    for pv, pp in ((HI, HI), (HI, LO), (LO, HI)):
                        for a in range(2):
                            h = 2 * pair + a
                            nc.tensor.matmul(AV[a * D:(a + 1) * D, 0, :], V[:, par, pv, c, h * D:(h + 1) * D],
                                             PT[:, g % 2, a, pp, c, :], start=(c == 0 and pv == pp),
                                             stop=(c == ST - 1 and pv == LO), tile_position=(0, a * D))
                if k == 3:
                    pe.wait_ge(rb_done, b * 16 + (g + 1))
                    for j in range(2):
                        for part in (HI, LO):
                            for a in range(2):
                                last = nc.tensor.matmul(AV[a * D:(a + 1) * D, 1, j * P:(j + 1) * P],
                                                        rb[:, part, 2 * j + a, :], id16[:],
                                                        start=(part == HI), stop=(part == LO),
                                                        tile_position=(0, a * D))
                    last.then_inc(av_done, 1)

            for r in range(2):
                for stage in range(2):
                    count_stage[0] = stage
                    group_average(2 * r + stage + 1, 0)
            pe.wait_ge(stat_read, 4)
            for F, item in enumerate(HEAD_START):
                for part_of in range(2):
                    filler(F, item, 0, 0, part_of)
            scores(0, 0, True)

            def batch(b, par, first, last):
                slots = slots_of(b, first, last)
                for i in range(STEPS):
                    if i + 1 < STEPS:
                        scores(b, i + 1, first)
                    elif not last:
                        scores(b + 1, 0, False)
                    s = i // 2
                    if s in slots:
                        item, off = slots[s]
                        if i % 2 == 0 and not last and i - 1 in MEAN_STEP + VAR_STEP:
                            r = (i - 1 > STAT_STEP[1]) * 1
                            pe.wait_ge(stat_read, b * 4 + (4 + 2 * r + (i - 1 in VAR_STEP) + 1))
                        filler(filler_number(b, s), item, b + off, (par + off) % 2, i % 2)
                    transposes(b, i)
                    if i in MEAN_STEP + VAR_STEP and not last:
                        r = (i > STAT_STEP[1]) * 1
                        stage = (i in VAR_STEP) * 1
                        count_stage[0] = stage
                        group_average(b * 4 + (4 + 2 * r + stage + 1),
                                      16 if first and s < 8 else filler_number(b, s) + 1)
                    g, k = i // 4 - 1, i % 4
                    if g >= 0:
                        weighted_sum(b, g, k, par)
                    elif not first:
                        weighted_sum(b - 1, 15, k, 1 - par)

            run_batches(pe, batch)
            for k in range(4):
                weighted_sum(B - 1, 15, k, 1)
            for s in range(8):
                for part_of in range(2):
                    filler(filler_number(B - 1, AHEAD + s), SLOTS[s], B - 1, 1, part_of)

        @block.scalar
        def _(act):
            for m in range(16):
                act.wait_ge(setup_pe, m + 2)
                dst = Wqkv[:, HI, :, m * P:(m + 1) * P] if m < 12 else Wp[:, HI, :, (m - 12) * P:(m - 11) * P]
                nc.scalar.activation(dst, wbank[:, m % 4], ACT.Copy).then_inc(w_hi, 1)

            def numerators(b, i):
                act.wait_ge(nb_done, b * STEPS + (i + 1))
                nc.scalar.activation(Pr[:], SC[:, i % 2, :], ACT.Exp, bias=nbias[:, i % 4:i % 4 + 1],
                                     scale=sscale[:, 0:1],
                                     accum_out=acc[:, (i // 4) % 2, i % 4:i % 4 + 1]).then_inc(e_done, 1)

            def copy_reciprocals(G, at_count):
                act.wait_ge(av_done, at_count + 1)
                wait(act, av_read, at_count)
                nc.scalar.activation(rsb[:], AV[:, 1, :], ACT.Copy).then_inc(r_copied, 1)

            numerators(0, 0)

            def batch(b, par, first, last):
                for i in range(STEPS):
                    g, k, a, j = i // 4, i % 4, i % 2, (i % 4) // 2
                    if k == 0 and not (first and g < 2):
                        copy_reciprocals(None, b * 16 + (g - 2))
                    act.wait_ge(t_done, b * STEPS + (i + 1))
                    if k == 0:
                        wait(act, av_done, b * 16 + (g - 1))
                    nc.scalar.activation(PT[:, g % 2, a, HI, :, j * P:(j + 1) * P], TP[:], ACT.Copy,
                                         scale=PS).then_inc(ph_done, 1)
                    if i + 1 < STEPS:
                        numerators(b, i + 1)
                    elif not last:
                        numerators(b + 1, 0)

            run_batches(act, batch)
            for G in (16 * B - 2, 16 * B - 1):
                copy_reciprocals(None, G)

        @block.vector
        def _(dve):
            v = nc.vector
            chain = Chain(dve, dve_chain)
            chain.per_batch = DVE_CHAIN
            dve.wait_ge(w_loaded, 16 * 16)
            gbb = gb.unsqueeze(1).to_broadcast([P, 12, C])
            gwb = gw.unsqueeze(1).to_broadcast([P, 12, C])
            chain(v.tensor_tensor(prod, wn, gbb, ALU.mult))
            chain(v.tensor_reduce(tmp[:], prod, AX.X, ALU.add))
            chain(v.tensor_tensor(bq[:], bq[:], tmp[:], ALU.add))
            chain(v.tensor_tensor(wn, wn, gwb, ALU.mult))
            chain(v.tensor_reduce(bound[:], wn, AX.X, ALU.add, apply_absolute_value=True))
            chain(v.tensor_scalar(tmp[:], bq[:], -1.0, None, ALU.mult))
            chain(v.tensor_tensor(tmp[:], tmp[:], bq[:], ALU.max))
            chain(v.scalar_tensor_tensor(bound[:], bound[:], XS, tmp[:], ALU.mult, ALU.add))
            chain(v.tensor_scalar(bound[:], bound[:], 1e-30, None, ALU.max))
            chain(v.memset(ones, 1.0))
            dve.wait_ge(consts, 3)
            for p in range(PAIRS):
                last = v.tensor_scalar(diag[:, p, :], id32[:], bound[:, 8 + p:9 + p], None, ALU.mult)
            last.then_inc(setup_dve, 1)
            chain(v.reciprocal(omega[:], bound[:]))
            chain(v.tensor_scalar(omega[:], omega[:], ROW * XS, None, ALU.mult))
            v.tensor_tensor(wn, wn, omega[:].unsqueeze(2).to_broadcast([P, 12, C]), ALU.mult) \
                .then_inc(setup_dve, 1)
            chain(v.tensor_reduce(top2[:], bound[:, 0:8].rearrange("p (k m) -> p k m", k=2), AX.X, ALU.max))
            dve.sem_inc(setup_pool, 1)
            dve.wait_ge(setup_pool, 2)
            chain(v.tensor_tensor(sscale[:], gtop[:, 0:1], gtop[:, 1:2], ALU.mult))
            chain(v.tensor_scalar(sscale[:], sscale[:], float(D) ** -0.5 / TOP ** 2, None, ALU.mult))
            chain(v.reciprocal(top2[:], gtop[:]))
            chain(v.tensor_scalar(top2[:], top2[:], TOP, None, ALU.mult))
            for k in range(2):
                m = slice(4 * k, 4 * k + 4)
                chain(v.tensor_scalar(cq[:, m], bound[:, m], top2[:, k:k + 1], 1.0 / (XS * ROW * XS),
                                      ALU.mult, ALU.mult))
                chain(v.tensor_scalar(bq[:, m], bq[:, m], top2[:, k:k + 1], None, ALU.mult))
            chain(v.tensor_scalar(tmp[:, 8:12], omega[:, 8:12], TOP / (ROW * XS), None, ALU.mult))
            chain(v.tensor_tensor(bq[:, 8:12], bq[:, 8:12], tmp[:, 8:12], ALU.mult))
            dve.wait_ge(setup_pe, 1)
            brow = AV[:].rearrange("p a t -> p (a t)").unsqueeze(1).to_broadcast([P, 4, C])
            chain(v.tensor_tensor(wpn, wpn, brow, ALU.mult))
            chain(v.tensor_reduce(cp[:], wpn, AX.X, ALU.add, apply_absolute_value=True))
            chain(v.tensor_scalar(cp[:], cp[:], 1e-30, None, ALU.max))
            chain(v.reciprocal(tmp[:, 0:4], cp[:]))
            chain(v.tensor_scalar(tmp[:, 0:4], tmp[:, 0:4], ROW, None, ALU.mult))
            chain(v.tensor_scalar(cp[:], cp[:], 1.0 / (ROW * TOP), None, ALU.mult))
            v.tensor_tensor(wpn, wpn, tmp[:, 0:4].unsqueeze(2).to_broadcast([P, 4, C]), ALU.mult) \
                .then_inc(setup_dve, 1)
            for m in range(16):
                dve.wait_ge(w_hi, m + 1)
                cols = slice(m * P, m * P + P) if m < 12 else slice((m - 12) * P, (m - 11) * P)
                W = Wqkv if m < 12 else Wp
                v.tensor_tensor(W[:, LO, :, cols], wbank[:, m % 4], W[:, HI, :, cols], ALU.subtract) \
                    .then_inc(w_lo, 1)

            def stats(X, r, n):
                c, half = n // 2, n % 2
                if half == 0:
                    dve.wait_ge(xc_loaded[c], X * 32 + 16 * (r + 1))
                chain.alone = half == 1
                chain(v.bn_stats(st6[:, c, half, :], xc[:, c, half * 512:half * 512 + 512]))
                chain.alone = False
                if half == 1:
                    ins = v.bn_aggr(mv[:, c, :], st6[:, c, :, :])
                    if c == 1:
                        chain(ins)
                        v.tensor_copy(dd[:], mv[:, :, 1]).then_inc(stat_in, 1)
                    else:
                        chain(ins)

            def group_mean(X, r):
                dve.wait_ge(stat_out, X * 4 + (2 * r + 1))
                wait(dve, xn_done, X * 4 + 2 * r)
                ins = v.tensor_copy(gm[:], FB[:, 0:2])
                ins.then_inc(stat_read, 1)
                dve.wait_ge(stat_read, X * 4 + (2 * r + 1))
                chain(v.tensor_tensor(ex[:], mv[:, :, 0], gm[:], ALU.subtract))
                chain(v.tensor_tensor(ex[:], ex[:], ex[:], ALU.mult))
                v.tensor_tensor(ex[:], ex[:], dd[:], ALU.add).then_inc(stat_in, 1)

            def rsqrt_steps(X, r):
                def read():
                    dve.wait_ge(stat_out, X * 4 + (2 * r + 2))
                    v.tensor_scalar(na[:], FB[:, 0:2], EPS, None, ALU.add).then_inc(stat_read, 1)
                    dve.wait_ge(stat_read, X * 4 + (2 * r + 2))

                def guess():
                    chain(v.tensor_scalar(hv[:], na[:], -0.5, None, ALU.mult))
                    chain(v.tensor_scalar(ny[:].bitcast(U32), na[:].bitcast(U32), 1, None,
                                          ALU.logical_shift_right))
                    chain(v.tensor_scalar(ny[:].bitcast(U32), ny[:].bitcast(U32), -1.0, 1597463007.0,
                                          ALU.mult, ALU.add))

                def newton():
                    chain(v.tensor_tensor(na[:], ny[:], ny[:], ALU.mult))
                    chain(v.tensor_tensor(na[:], na[:], hv[:], ALU.mult))
                    chain(v.scalar_tensor_tensor(ny[:], na[:], 1.5, ny[:], ALU.add, ALU.mult))

                def scaled():
                    v.tensor_scalar(rs[:], ny[:], XS, None, ALU.mult).then_inc(norm_ready, 1)

                return [(read, guess), (newton, newton), (newton, newton, scaled)]

            def scaled_filler(F, item):
                kind, i0, i1 = item
                dve.wait_ge(filler_psum, F + 1)
                wait(dve, filler_out, F)
                if kind == "v":
                    ins = v.tensor_scalar(yf[:], FB[:], TOP / (XS * ROW * XS), None, ALU.mult)
                elif kind == "qk":
                    m = (i1 // 2) * 4 + i0
                    ins = v.tensor_scalar(yf[:], FB[:], cq[:, m:m + 1], bq[:, m:m + 1], ALU.mult, ALU.add)
                else:
                    ins = v.tensor_scalar(yf[:], FB[:], cp[:, i1:i1 + 1], bp[:, i1:i1 + 1], ALU.mult, ALU.add)
                ins.then_inc(y_done, 1)

            def row_max(b, i):
                dve.wait_ge(s_done, b * STEPS + (i + 1))
                q = i % 4
                chain(v.tensor_reduce(nmax[:, q:q + 1], SC[:, i % 2, :], AX.X, ALU.max, negate=True))
                v.tensor_scalar(nbias[:, q:q + 1], nmax[:, q:q + 1], sscale[:, 0:1], None, ALU.mult) \
                    .then_inc(nb_done, 1)

            def normalised_outputs(count):
                dve.wait_ge(r_copied, count + 1)
                wait(dve, at_done, count)
                v.scalar_tensor_tensor(at[:], AV[:, 0, :], 1.0 / (PS * RS), rsb[:], ALU.mult, ALU.mult) \
                    .then_inc(av_read, 1)

            def reciprocals(count, gpar):
                dve.wait_ge(e_done, (count + 1) * 4)
                wait(dve, rb_done, count - 1)
                v.reciprocal(rinv[:, gpar, :], acc[:, gpar, :]).then_inc(ri_done, 1)

            for r in range(2):
                for n in range(4):
                    stats(0, r, n)
                group_mean(0, r)
                for stp in rsqrt_steps(0, r):
                    for f in stp:
                        f()
            for F, item in enumerate(HEAD_START):
                scaled_filler(F, item)
            row_max(0, 0)

            def batch(b, par, first, last):
                slots = slots_of(b, first, last)
                for i in range(STEPS):
                    g, k, a, j = i // 4, i % 4, i % 2, (i % 4) // 2
                    if i + 1 < STEPS:
                        row_max(b, i + 1)
                    elif not last:
                        row_max(b + 1, 0)
                    if i % 2 == 1 and i // 2 in slots:
                        scaled_filler(filler_number(b, i // 2), slots[i // 2][0])
                    if k == 0:
                        if not (first and g < 2):
                            normalised_outputs(b * 16 + (g - 2))
                        if not (first and g < 1):
                            reciprocals(b * 16 + (g - 1), (g - 1) % 2)
                    dve.wait_ge(ph_done, b * STEPS + (i + 1))
                    v.scalar_tensor_tensor(PT[:, g % 2, a, LO, :, j * P:(j + 1) * P], TP[:], PS,
                                           PT[:, g % 2, a, HI, :, j * P:(j + 1) * P],
                                           ALU.mult, ALU.subtract).then_inc(pl_done, 1)
                    if not last:
                        for r in range(2):
                            if 0 <= i - STAT_STEP[r] < 4:
                                stats(b + 1, r, i - STAT_STEP[r])
                            if i == MEAN_STEP[r]:
                                group_mean(b + 1, r)
                            if 0 <= i - VAR_STEP[r] < 3:
                                for f in rsqrt_steps(b + 1, r)[i - VAR_STEP[r]]:
                                    f()

            run_batches(dve, batch, chain)
            normalised_outputs(16 * B - 2)
            reciprocals(16 * B - 1, 1)
            normalised_outputs(16 * B - 1)
            for s in range(8):
                scaled_filler(filler_number(B - 1, AHEAD + s), SLOTS[s])

        @block.gpsimd
        def _(pool):
            v = nc.gpsimd
            chain = Chain(pool, pool_chain)
            chain.per_batch = POOL_CHAIN
            chain(v.memset(id32[:], 0.0))
            v.affine_select(out=id32[:], in_=id32[:], compare_op=ALU.not_equal, fill=1.0, base=0,
                            pattern=[[-1, P]], channel_multiplier=1).then_inc(consts, 1)
            chain(v.memset(id16[:], 0.0))
            v.affine_select(out=id16[:], in_=id16[:], compare_op=ALU.not_equal, fill=1.0, base=0,
                            pattern=[[-1, P]], channel_multiplier=1).then_inc(consts, 1)
            chain(v.memset(gavg[:], 1.0 / CPG))
            gv = gavg[:].rearrange("p (g c) -> p g c", c=CPG)
            chain(v.affine_select(out=gv, in_=gv, compare_op=ALU.is_ge, fill=0.0, base=0,
                                  pattern=[[-CPG, P // CPG], [0, CPG]], channel_multiplier=1))
            v.affine_select(out=gv, in_=gv, compare_op=ALU.is_ge, fill=0.0, base=CPG - 1,
                            pattern=[[CPG, P // CPG], [0, CPG]], channel_multiplier=-1).then_inc(consts, 1)
            chain.alone = True
            pool.wait_ge(setup_pool, 1)
            v.partition_all_reduce(gtop[:], top2[:], P, RMAX).then_inc(setup_pool, 1)

            def normalise(X, par, r, n):
                c, op = n // 3, n % 3
                kc = 2 * r + c
                if op == 0:
                    if c == 0:
                        apart(pool, X * 2 + (r + 1), *([(X - 2) * 32 + 24] if r == 0 else []))
                        pool.wait_ge(norm_ready, X * 2 + (r + 1))
                    if c == 0 and r == 0:
                        wait(pool, filler_psum, (X - 2) * 32 + 24)
                    chain(v.tensor_scalar(xc[:, c, :], xc[:, c, :], gm[:, c:c + 1], rs[:, c:c + 1],
                                          ALU.subtract, ALU.mult))
                elif op == 1:
                    chain(v.tensor_copy(XN[:, par, HI, kc, :], xc[:, c, :]))
                else:
                    v.tensor_tensor(XN[:, par, LO, kc, :], xc[:, c, :], XN[:, par, HI, kc, :],
                                    ALU.subtract).then_inc(xn_done, 1)

            def use_filler(F, item, b, par):
                kind, i0, i1 = item
                i, half = 4 * i0 + i1, i1 % 2
                copied = b * (192 * PAIRS) + (192 * i0 + (64 if i1 >= 2 else 0))
                apart(pool, F + 1, {"proj": b * 64 + 16 * (i // 2 + 1), "v": (b - 1) * 16, "qk": copied}[kind])
                pool.wait_ge(y_done, F + 1)
                if kind == "proj":
                    pool.wait_ge(res_loaded[i % 2], b * 64 + 16 * (i // 2 + 1))
                    v.tensor_tensor(xres[:, i % 2, :], xres[:, i % 2, :], yf[:], ALU.add) \
                        .then_inc(filler_out, 1)
                    return
                if kind == "v":
                    hi, lo = V[:, par, HI, i0, :], V[:, par, LO, i0, :]
                    if i0 == 0:
                        wait(pool, av_done, (b - 1) * 16)
                else:
                    hi, lo = nat[:, half, HI, :], nat[:, half, LO, :]
                    wait(pool, stacked[half], copied)
                chain(v.tensor_copy(hi, yf[:]))
                v.tensor_tensor(lo, yf[:], hi, ALU.subtract).then_inc(filler_out, 1)

            def reciprocal_parts(count, gpar):
                apart(pool, count + 1, count)
                pool.wait_ge(ri_done, count + 1)
                wait(pool, av_done, count)
                chain(v.tensor_scalar(rscl[:], rinv[:, gpar, :], RS, None, ALU.mult))
                wide = rscl[:].unsqueeze(2).to_broadcast([P, 4, D])
                chain(v.tensor_copy(rb[:, HI], wide))
                v.tensor_tensor(rb[:, LO], wide, rb[:, HI], ALU.subtract).then_inc(rb_done, 1)

            def output_parts(count, g, be):
                pair, u = g // 4, g % 4
                apart(pool, count + 1, be * 32 + (12 + 4 * (u // 2)))
                pool.wait_ge(av_read, count + 1)
                if not (isinstance(be, int) and be == 0):
                    pool.wait_ge(filler_psum, be * 32 + (12 + 4 * (u // 2)))
                cols = slice(u * TG, (u + 1) * TG)
                chain(v.tensor_scalar(at[:], at[:], bq[:, 8 + pair:9 + pair], None, ALU.add))
                chain(v.tensor_copy(AT[:, HI, pair, cols], at[:]))
                v.tensor_tensor(AT[:, LO, pair, cols], at[:], AT[:, HI, pair, cols], ALU.subtract) \
                    .then_inc(at_done, 1)

            for r in range(2):
                for n in range(6):
                    normalise(0, 0, r, n)
            for F, item in enumerate(HEAD_START):
                use_filler(F, item, 0, 0)

            def batch(b, par, first, last):
                slots = slots_of(b, first, last)
                for i in range(STEPS):
                    g, k = i // 4, i % 4
                    if i % 2 == 1 and i // 2 in slots:
                        item, off = slots[i // 2]
                        use_filler(filler_number(b, i // 2), item, b + off, (par + off) % 2)
                    if k == 0 and not (first and g < 1):
                        reciprocal_parts(b * 16 + (g - 1), (g - 1) % 2)
                    if k == 1 and not (first and g < 2):
                        output_parts(b * 16 + (g - 2), (g - 2) % 16, b if g >= 2 else b - 1)
                    if not last:
                        for r in range(2):
                            if 0 <= i - NORM_STEP[r] < 6:
                                normalise(b + 1, 1 - par, r, i - NORM_STEP[r])

            run_batches(pool, batch, chain)
            output_parts(16 * B - 2, 14, B - 1)
            reciprocal_parts(16 * B - 1, 1)
            output_parts(16 * B - 1, 15, B - 1)
            for s in range(8):
                use_filler(filler_number(B - 1, AHEAD + s), SLOTS[s], B - 1, 1)


DVE_CHAIN = 110
POOL_CHAIN = 96

_INS = ["x", "L0_conv_gn_w", "L0_conv_gn_b", "L0_conv_qkv_w", "L0_conv_qkv_b", "L0_conv_proj_w", "L0_conv_proj_b"]


def kernel(**inputs):
    import numpy as _np
    import concourse.bacc as _bacc
    from concourse import mybir as _mybir
    from concourse.bass_utils import run_bass_kernel_spmd as _run

    nc = _bacc.Bacc("TRN2", target_bir_lowering=False, num_devices=1)
    arrays, args = {}, []
    for name in _INS:
        a = _np.ascontiguousarray(inputs[name])
        arrays[f"in_{name}_dram"] = a
        args.append(nc.dram_tensor(f"in_{name}_dram", a.shape, _mybir.dt.from_np(a.dtype), kind="ExternalInput").ap())
    shape = inputs["x"].shape
    args.append(nc.dram_tensor("out_dram", shape, _mybir.dt.from_np(_np.dtype("float32")), kind="ExternalOutput").ap())
    bass_groupnorm_attention_kernel(nc, *args)
    r = _run(nc, [arrays], core_ids=[0])
    return r.results[0]["out_dram"]
```

```python
from contextlib import ExitStack

import concourse.bass as bass
from concourse import mybir

F32 = mybir.dt.float32
F16 = mybir.dt.float16
U32 = mybir.dt.uint32
ALU = mybir.AluOpType
ACT = mybir.ActivationFunctionType
AX = mybir.AxisListType
RMAX = bass.bass_isa.ReduceOp.max

P = 128
HEADS = 8
GROUPS = 32
EPS = 1e-5
HI, LO = 0, 1

XS = 2.0 ** 7
ROW = 2.0 ** 14
TOP = 2.0 ** 15
PS = 2.0 ** 14
RS = 2.0 ** 14

SLOTS = ([("proj", n, m) for n in range(2) for m in range(4)]
         + [("qk", 2, n) for n in range(4)] + [("qk", 3, n) for n in range(4)]
         + [("v", s, 0) for s in range(8)]
         + [("qk", 0, n) for n in range(4)] + [("qk", 1, n) for n in range(4)])
AHEAD = 16
HEAD_START = SLOTS[AHEAD:]
STACK = [0, 1, 0, 2]

SUM_STEP = [1, 16]
MEAN_STEP = [5, 19]
SQUARE_STEP = [6, 20]
VAR_STEP = [9, 23]
RSQRT_STEP = [10, 24]
NORM_STEP = [11, 26]
PARTS_STEP = [13, 28]


def filler_number(b, slot):
    return b * 32 + 8 + slot


def bass_groupnorm_attention_kernel(nc, x, gn_w, gn_b, qkv_w, qkv_b, proj_w, proj_b, out):
    B, C, HH, WW = x.shape
    T = HH * WW
    D = C // HEADS
    KC = C // P
    PAIRS = HEADS // 2
    ST = T // P
    STEPS = HEADS * ST
    TG = 2 * P
    CPG = C // GROUPS
    assert (C, T, D, KC, STEPS, CPG) == (512, 1024, 64, 4, 64, 16) and B % 2 == 0
    assert CPG * T == 2 ** 14

    xr_v = x.rearrange("b c h w -> b c (h w)")
    out_v = out.rearrange("b c h w -> b c (h w)")

    with ExitStack() as ctx:
        def sb(name, shape, dt):
            return ctx.enter_context(nc.sbuf_tensor(name, shape, dt))

        def sem(name):
            return ctx.enter_context(nc.semaphore(name))

        Wqkv = sb("Wqkv", [P, 2, KC, 3 * C], F16)
        Wp = sb("Wp", [P, 2, KC, C], F16)
        XN = sb("XN", [P, 2, 2, KC, T], F16)
        xc = sb("xc", [P, 2, T], F32)
        V = sb("V", [P, 2, 2, ST, C], F16)
        PT = sb("PT", [P, 2, 2, 2, ST, TG], F16)
        Pr = sb("Pr", [P, T], F32)
        yf = sb("yf", [P, 512], F32)
        nat = sb("nat", [P, 2, 2, 512], F16)
        QS = sb("QS", [P, 3, 2, T], F16)
        KH = sb("KH", [P, 3, 2, T], F16)
        KL = sb("KL", [P, 3, 2, T], F16)
        AT = sb("AT", [P, 2, KC, T], F16)
        rsb = sb("rsb", [P, TG], F32)
        at = sb("at", [P, TG], F32)
        xres = sb("xres", [P, 2, 512], F32)
        id32 = sb("id32", [P, P], F32)
        id16 = sb("id16", [P, P], F16)
        gavg = sb("gavg", [P, P], F32)
        rb = sb("rb", [P, 2, 4, D], F16)
        acc = sb("acc", [P, 2, 4], F32)
        rinv = sb("rinv", [P, 2, 4], F32)
        rscl = sb("rscl", [P, 4], F32)
        nmax = sb("nmax", [P, 4], F32)
        nbias = sb("nbias", [P, 4], F32)
        sscale = sb("sscale", [P, 1], F32)
        cq = sb("cq", [P, 12], F32)
        bq = sb("bq", [P, 12], F32)
        cp = sb("cp", [P, 4], F32)
        bp = sb("bp", [P, 4], F32)
        sums = sb("sums", [P, 2, 2], F32)
        ngm = sb("ngm", [P, 2], F32)
        rs = sb("rs", [P, 2], F32)
        hv = sb("hv", [P, 2], F32)
        ny = sb("ny", [P, 2], F32)
        na = sb("na", [P, 2], F32)
        bound = sb("bound", [P, 12], F32)
        tmp = sb("tmp", [P, 12], F32)
        omega = sb("omega", [P, 12], F32)
        top2 = sb("top2", [P, 2], F32)
        gtop = sb("gtop", [P, 2], F32)

        borrowed = PT[:].rearrange("p a b c d e -> p (a b c d e)").bitcast(F32)
        wn = borrowed[:, 0:12 * C].rearrange("p (m c) -> p m c", c=C)
        wpn = borrowed[:, 12 * C:16 * C].rearrange("p (m c) -> p m c", c=C)
        borrowed_v = V[:].rearrange("p a b c d -> p (a b c d)").bitcast(F32)
        prod = borrowed_v[:, 0:12 * C].rearrange("p (m c) -> p m c", c=C)
        gw = borrowed_v[:, 12 * C:13 * C]
        gb = borrowed_v[:, 13 * C:14 * C]
        diag = borrowed_v[:, 14 * C:15 * C].rearrange("p (m c) -> p m c", c=P)
        ones = borrowed_v[:, 15 * C:15 * C + P]

        SC = ctx.enter_context(nc.psum_tensor("SC", [P, 2, T], F32))
        TP = ctx.enter_context(nc.psum_tensor("TP", [P, ST, P], F32))
        AV = ctx.enter_context(nc.psum_tensor("AV", [P, 2, TG], F32))
        FB = ctx.enter_context(nc.psum_tensor("FB", [P, 512], F32))
        wbank = SC[:].rearrange("p a (b m c) -> p (a b) m c", b=2, c=P)

        w_loaded = sem("w_loaded")
        consts = sem("consts")
        setup_pool = sem("setup_pool")
        setup_dve = sem("setup_dve")
        setup_pe = sem("setup_pe")
        w_hi = sem("w_hi")
        w_lo = sem("w_lo")
        xc_loaded = [sem(f"xc_loaded{c}") for c in range(2)]
        res_loaded = [sem(f"res_loaded{c}") for c in range(2)]
        stored = [sem(f"stored{c}") for c in range(2)]
        stacked = [sem(f"stacked{c}") for c in range(2)]
        stat_in = sem("stat_in")
        stat_out = sem("stat_out")
        stat_read = sem("stat_read")
        guessed = sem("guessed")
        norm_ready = sem("norm_ready")
        xy_done = sem("xy_done")
        xn_done = sem("xn_done")
        s_done = sem("s_done")
        nb_done = sem("nb_done")
        e_done = sem("e_done")
        t_done = sem("t_done")
        ph_done = sem("ph_done")
        xh_done = sem("xh_done")
        yh_done = sem("yh_done")
        ah_done = sem("ah_done")
        pl_done = sem("pl_done")
        ri_done = sem("ri_done")
        rb_done = sem("rb_done")
        av_done = sem("av_done")
        r_copied = sem("r_copied")
        av_read = sem("av_read")
        at_done = sem("at_done")
        filler_psum = sem("filler_psum")
        y_done = sem("y_done")
        filler_out = sem("filler_out")
        dve_chain = sem("dve_chain")
        pool_chain = sem("pool_chain")

        block = ctx.enter_context(nc.Block())

        def wait(eng, s, value):
            if not isinstance(value, int) or value > 0:
                eng.wait_ge(s, value)

        def apart(eng, *values):
            for value in values:
                if not isinstance(value, int):
                    eng.compute_val(value)
            eng.wait_ge(consts, 3)

        class Chain:

            def __init__(self, eng, s):
                self.eng, self.sem, self.base, self.n, self.alone = eng, s, 0, 0, False

            def __call__(self, ins):
                self.n += 1
                ins.then_inc(self.sem, 1)
                if self.alone:
                    apart(self.eng, self.base + self.n)
                self.eng.wait_ge(self.sem, self.base + self.n)

        def run_batches(eng, batch, chain=None):
            batch(0, 0, True, False)
            if chain:
                before = chain.n
            with eng.Fori(0, B // 2 - 1) as j:
                if chain:
                    chain.base, chain.n = before + j * (2 * chain.per_batch), 0
                batch(j * 2 + 1, 1, False, False)
                batch(j * 2 + 2, 0, False, False)
                if chain:
                    assert chain.n == 2 * chain.per_batch, (chain.n, chain.per_batch)
            if chain:
                chain.base, chain.n = 0, before + (B - 2) * chain.per_batch
            batch(B - 1, 1, False, True)

        def slots_of(b, first, last):
            found = {}
            for s, item in enumerate(SLOTS):
                if first and s < 8 or last and s >= AHEAD:
                    continue
                found[s] = (item, -1 if item[0] == "proj" else 1 if s >= AHEAD else 0)
            return found

        @block.sync
        def _(sp):
            for a in range(2):
                for kind in range(3):
                    src = qkv_w.rearrange("(q a k r) c -> a k r q c", a=2, k=3, r=D)[a, kind]
                    sp.dma_start(wn[a * D:(a + 1) * D, kind * 4:kind * 4 + 4, :], src).then_inc(w_loaded, 16)
                    bsrc = qkv_b.rearrange("(q a k r) -> a k r q", a=2, k=3, r=D)[a, kind]
                    sp.dma_start(bq[a * D:(a + 1) * D, kind * 4:kind * 4 + 4], bsrc,
                                 allow_slow_non_contiguous=True).then_inc(w_loaded, 16)
            sp.dma_start(wpn, proj_w.rearrange("(m p) c -> p m c", p=P)).then_inc(w_loaded, 16)
            sp.dma_start(bp[:], proj_b.rearrange("(m p) -> p m", p=P), allow_slow_non_contiguous=True).then_inc(w_loaded, 16)
            sp.dma_start(gw, gn_w.partition_broadcast(P)).then_inc(w_loaded, 16)
            sp.dma_start(gb, gn_b.partition_broadcast(P)).then_inc(w_loaded, 16)

            def load_chunks(X, r):
                for c in range(2):
                    apart(sp, X * 4 + (2 * r + c - 1))
                    wait(sp, xn_done, X * 4 + (2 * r + c - 1))
                    kc = 2 * r + c
                    sp.dma_start(xc[:, c, :], xr_v[X, kc * P:(kc + 1) * P, :]).then_inc(xc_loaded[c], 16)

            def load_residual(b, i):
                n, m = i // 4, i % 4
                sp.dma_start(xres[:, i % 2, :], xr_v[b, m * P:(m + 1) * P, n * 512:(n + 1) * 512]) \
                    .then_inc(res_loaded[i % 2], 16)

            def store(b, i, F):
                n, m = i // 4, i % 4
                apart(sp, F + 1)
                sp.wait_ge(filler_out, F + 1)
                sp.dma_start(out_v[b, m * P:(m + 1) * P, n * 512:(n + 1) * 512], xres[:, i % 2, :]) \
                    .then_inc(stored[i % 2], 16)
                apart(sp, b * 64 + 16 * (i // 2 + 1))
                sp.wait_ge(stored[i % 2], b * 64 + 16 * (i // 2 + 1))

            def stack_qk(b, pair, n, F):
                kind, half = n // 2, n % 2
                cols = slice(half * 512, half * 512 + 512)
                buf = STACK[pair]
                scored = b * STEPS + [-16, -32, 16, 0][pair]
                apart(sp, F + 1, scored)
                sp.wait_ge(filler_out, F + 1)
                wait(sp, s_done, scored)
                for a in range(2):
                    rows = slice(a * D, a * D + D)
                    if kind == 0:
                        for part in (HI, LO):
                            sp.dma_start(QS[part * D:part * D + D, buf, a, cols], nat[rows, half, part, :]) \
                                .then_inc(stacked[half], 16)
                    else:
                        for part, dst in ((HI, KH), (LO, KL)):
                            for z in range(2):
                                sp.dma_start(dst[z * D:z * D + D, buf, a, cols], nat[rows, half, part, :]) \
                                    .then_inc(stacked[half], 16)

            load_chunks(0, 0)
            load_chunks(0, 1)
            for i in range(2):
                load_residual(0, i)
            for F, item in enumerate(HEAD_START):
                if item[0] == "qk":
                    stack_qk(0, item[1], item[2], F)

            def batch(b, par, first, last):
                if not last:
                    load_chunks(b + 1, 0)
                for s, (item, off) in slots_of(b, first, last).items():
                    F = filler_number(b, s)
                    if s == 8 and not last:
                        load_chunks(b + 1, 1)
                    if item[0] == "proj":
                        store(b - 1, s, F)
                        load_residual(b - 1 if s < 6 else b, (s + 2) % 8)
                    if item[0] == "qk":
                        stack_qk(b + off, item[1], item[2], F)

            run_batches(sp, batch)
            for s in range(8):
                store(B - 1, s, filler_number(B - 1, AHEAD + s))
                if s < 6:
                    load_residual(B - 1, s + 2)

        @block.tensor
        def _(pe):
            pe.wait_ge(consts, 3)
            pe.wait_ge(setup_dve, 1)
            nc.tensor.matmul(AV[:].rearrange("p a t -> p (a t)"), ones, diag.rearrange("p m c -> p (m c)"),
                             start=True, stop=True).then_inc(setup_pe, 1)
            for m in range(16):
                if m >= 4:
                    pe.wait_ge(w_lo, m - 3)
                if m == 0:
                    pe.wait_ge(setup_dve, 2)
                if m == 12:
                    pe.wait_ge(setup_dve, 3)
                src = wn[:, m, :] if m < 12 else wpn[:, m - 12, :]
                for kc in range(KC):
                    last = nc.tensor.transpose(wbank[:, m % 4, kc, :], src[:, kc * P:(kc + 1) * P], id32[:])
                last.then_inc(setup_pe, 1)

            def filler(F, item, b, par, part_of):
                kind, i0, i1 = item
                if part_of == 0:
                    wait(pe, y_done, F)
                    if kind == "v" and i0 == 0:
                        pe.wait_ge(xn_done, b * 4 + 4)
                    if kind == "proj" and i1 == 0:
                        pe.wait_ge(at_done, b * 16 + (14 if i0 == 0 else 16))
                for kc in (0, 1) if part_of == 0 else (2, 3):
                    for ps, pm in ((HI, HI), (HI, LO), (LO, HI)):
                        if kind == "qk":
                            m = (i1 // 2) * 4 + i0
                            lhsT = Wqkv[:, ps, kc, m * P:(m + 1) * P]
                            rhs = XN[:, par, pm, kc, (i1 % 2) * 512:(i1 % 2) * 512 + 512]
                        elif kind == "v":
                            lhsT = XN[:, par, ps, kc, i0 * P:(i0 + 1) * P]
                            rhs = Wqkv[:, pm, kc, 2 * C:3 * C]
                        else:
                            lhsT = Wp[:, ps, kc, i1 * P:(i1 + 1) * P]
                            rhs = AT[:, pm, kc, i0 * 512:i0 * 512 + 512]
                        last = nc.tensor.matmul(FB[:], lhsT, rhs, start=(kc == 0 and ps == pm),
                                                stop=(kc == 3 and ps == LO))
                if part_of == 1:
                    last.then_inc(filler_psum, 1)

            def group_average(count, stage, fillers_before):
                wait(pe, y_done, fillers_before)
                pe.wait_ge(stat_in, count)
                nc.tensor.matmul(FB[:, 0:2], gavg[:], sums[:, stage, :], start=True, stop=True) \
                    .then_inc(stat_out, 1)

            def scores(b, i, first_tile):
                pair, u, j, a = i // 16, (i // 4) % 4, (i % 4) // 2, i % 2
                t0 = (2 * u + j) * P
                if i % 16 == 0:
                    for half in range(2):
                        pe.wait_ge(stacked[half], b * (192 * PAIRS) + 192 * (pair + 1))
                if not (first_tile and i < 2):
                    pe.wait_ge(e_done, b * STEPS + (i - 1))
                for half in range(2):
                    for K, start in ((KH, True), (KL, False)):
                        last = nc.tensor.matmul(SC[:, i % 2, half * 512:half * 512 + 512],
                                                QS[:, STACK[pair], a, t0:t0 + P],
                                                K[:, STACK[pair], a, half * 512:half * 512 + 512],
                                                start=start, stop=not start)
                last.then_inc(s_done, 1)

            def transposes(b, i):
                pe.wait_ge(e_done, b * STEPS + (i + 1))
                wait(pe, pl_done, b * STEPS + i)
                for c in range(ST):
                    last = nc.tensor.transpose(TP[:, c, :], Pr[:, c * P:(c + 1) * P], id32[:])
                last.then_inc(t_done, 1)

            def weighted_sum(b, g, k, par):
                pair = g // 4
                if k == 0:
                    pe.wait_ge(pl_done, b * STEPS + 4 * (g + 1))
                    wait(pe, av_read, b * 16 + g)
                    if g == 0:
                        pe.wait_ge(filler_out, 8 if isinstance(b, int) and b == 0 else b * 32)
                for c in (2 * k, 2 * k + 1):
                    for pv, pp in ((HI, HI), (HI, LO), (LO, HI)):
                        for a in range(2):
                            h = 2 * pair + a
                            nc.tensor.matmul(AV[a * D:(a + 1) * D, 0, :], V[:, par, pv, c, h * D:(h + 1) * D],
                                             PT[:, g % 2, a, pp, c, :], start=(c == 0 and pv == pp),
                                             stop=(c == ST - 1 and pv == LO), tile_position=(0, a * D))
                if k == 3:
                    pe.wait_ge(rb_done, b * 16 + (g + 1))
                    for j in range(2):
                        for part in (HI, LO):
                            for a in range(2):
                                last = nc.tensor.matmul(AV[a * D:(a + 1) * D, 1, j * P:(j + 1) * P],
                                                        rb[:, part, 2 * j + a, :], id16[:],
                                                        start=(part == HI), stop=(part == LO),
                                                        tile_position=(0, a * D))
                    last.then_inc(av_done, 1)

            for r in range(2):
                for stage in range(2):
                    if r + stage:
                        pe.wait_ge(stat_read, 2 * r + stage)
                    group_average(2 * r + stage + 1, stage, 0)
            pe.wait_ge(stat_read, 4)
            for F, item in enumerate(HEAD_START):
                for part_of in range(2):
                    filler(F, item, 0, 0, part_of)
            scores(0, 0, True)

            def batch(b, par, first, last):
                slots = slots_of(b, first, last)
                for i in range(STEPS):
                    if i + 1 < STEPS:
                        scores(b, i + 1, first)
                    elif not last:
                        scores(b + 1, 0, False)
                    s = i // 2
                    if s in slots:
                        item, off = slots[s]
                        if i % 2 == 0 and not last and i - 1 in MEAN_STEP + VAR_STEP:
                            r = (i - 1 > SUM_STEP[1]) * 1
                            pe.wait_ge(stat_read, b * 4 + (4 + 2 * r + (i - 1 in VAR_STEP) + 1))
                        filler(filler_number(b, s), item, b + off, (par + off) % 2, i % 2)
                    transposes(b, i)
                    if i in MEAN_STEP + VAR_STEP and not last:
                        r = (i > SUM_STEP[1]) * 1
                        stage = (i in VAR_STEP) * 1
                        group_average(b * 4 + (4 + 2 * r + stage + 1), stage,
                                      16 if first and s < 8 else filler_number(b, s) + 1)
                    g, k = i // 4 - 1, i % 4
                    if g >= 0:
                        weighted_sum(b, g, k, par)
                    elif not first:
                        weighted_sum(b - 1, 15, k, 1 - par)

            run_batches(pe, batch)
            for k in range(4):
                weighted_sum(B - 1, 15, k, 1)
            for s in range(8):
                for part_of in range(2):
                    filler(filler_number(B - 1, AHEAD + s), SLOTS[s], B - 1, 1, part_of)

        @block.scalar
        def _(act):
            for m in range(16):
                act.wait_ge(setup_pe, m + 2)
                dst = Wqkv[:, HI, :, m * P:(m + 1) * P] if m < 12 else Wp[:, HI, :, (m - 12) * P:(m - 11) * P]
                nc.scalar.activation(dst, wbank[:, m % 4], ACT.Copy).then_inc(w_hi, 1)

            def numerators(b, i):
                act.wait_ge(nb_done, b * STEPS + (i + 1))
                nc.scalar.activation(Pr[:], SC[:, i % 2, :], ACT.Exp, bias=nbias[:, i % 4:i % 4 + 1],
                                     scale=sscale[:, 0:1],
                                     accum_out=acc[:, (i // 4) % 2, i % 4:i % 4 + 1]).then_inc(e_done, 1)

            def copy_reciprocals(count):
                act.wait_ge(av_done, count + 1)
                wait(act, av_read, count)
                nc.scalar.activation(rsb[:], AV[:, 1, :], ACT.Copy).then_inc(r_copied, 1)

            def sum_pass(X, par, r, stage, c):
                kc = 2 * r + c
                if stage == 0:
                    act.wait_ge(xc_loaded[c], X * 32 + 16 * (r + 1))
                    if kc == 0:
                        wait(act, filler_psum, (X - 2) * 32 + 24)
                elif c == 0:
                    act.wait_ge(stat_read, X * 4 + (2 * r + 1))
                ins = nc.scalar.activation(XN[:, par, HI, kc, :], xc[:, c, :],
                                           ACT.Square if stage else ACT.Identity,
                                           bias=ngm[:, c:c + 1] if stage else 0.0,
                                           accum_out=sums[:, stage, c:c + 1])
                if c == 1:
                    ins.then_inc(stat_in, 1)

            def normalised_hi(X, par, r, c):
                kc = 2 * r + c
                act.wait_ge(xy_done, X * 4 + (kc + 1))
                nc.scalar.activation(XN[:, par, HI, kc, :], xc[:, c, :], ACT.Copy).then_inc(xh_done, 1)

            def filler_hi(F, item, b, par):
                kind, i0, i1 = item
                if kind == "proj":
                    return
                act.wait_ge(y_done, F + 1)
                if kind == "v":
                    hi = V[:, par, HI, i0, :]
                    if i0 == 0:
                        wait(act, av_done, (b - 1) * 16)
                else:
                    half = i1 % 2
                    hi = nat[:, half, HI, :]
                    wait(act, stacked[half], b * (192 * PAIRS) + (192 * i0 + (64 if i1 >= 2 else 0)))
                nc.scalar.activation(hi, yf[:], ACT.Copy).then_inc(yh_done, 1)

            def outputs_hi(count, g, be):
                pair, u = g // 4, g % 4
                act.wait_ge(av_read, count + 1)
                if not (isinstance(be, int) and be == 0):
                    act.wait_ge(filler_psum, be * 32 + (12 + 4 * (u // 2)))
                nc.scalar.activation(AT[:, HI, pair, u * TG:(u + 1) * TG], at[:], ACT.Identity,
                                     bias=bq[:, 8 + pair:9 + pair]).then_inc(ah_done, 1)

            for r in range(2):
                for stage in range(2):
                    for c in range(2):
                        sum_pass(0, 0, r, stage, c)
                for c in range(2):
                    normalised_hi(0, 0, r, c)
            for F, item in enumerate(HEAD_START):
                filler_hi(F, item, 0, 0)
            numerators(0, 0)

            def batch(b, par, first, last):
                slots = slots_of(b, first, last)
                for i in range(STEPS):
                    g, k, a, j = i // 4, i % 4, i % 2, (i % 4) // 2
                    if k == 0 and not (first and g < 2):
                        copy_reciprocals(b * 16 + (g - 2))
                    act.wait_ge(t_done, b * STEPS + (i + 1))
                    if k == 0:
                        wait(act, av_done, b * 16 + (g - 1))
                    nc.scalar.activation(PT[:, g % 2, a, HI, :, j * P:(j + 1) * P], TP[:], ACT.Copy,
                                         scale=PS).then_inc(ph_done, 1)
                    if i + 1 < STEPS:
                        numerators(b, i + 1)
                    elif not last:
                        numerators(b + 1, 0)
                    if i % 2 == 1 and i // 2 in slots:
                        item, off = slots[i // 2]
                        filler_hi(filler_number(b, i // 2), item, b + off, (par + off) % 2)
                    if k == 0 and not (first and g < 2):
                        outputs_hi(b * 16 + (g - 2), (g - 2) % 16, b if g >= 2 else b - 1)
                    for r in range(2):
                        for c in range(2):
                            if i == SUM_STEP[r] + c and not last:
                                sum_pass(b + 1, 1 - par, r, 0, c)
                            if i == SQUARE_STEP[r] + c and not last:
                                sum_pass(b + 1, 1 - par, r, 1, c)
                            if i == PARTS_STEP[r] + c and not last:
                                normalised_hi(b + 1, 1 - par, r, c)

            run_batches(act, batch)
            for G in (16 * B - 2, 16 * B - 1):
                copy_reciprocals(G)
                outputs_hi(G, G % 16, B - 1)

        @block.vector
        def _(dve):
            v = nc.vector
            chain = Chain(dve, dve_chain)
            chain.per_batch = DVE_CHAIN
            dve.wait_ge(w_loaded, 16 * 16)
            gbb = gb.unsqueeze(1).to_broadcast([P, 12, C])
            gwb = gw.unsqueeze(1).to_broadcast([P, 12, C])
            chain(v.tensor_tensor(prod, wn, gbb, ALU.mult))
            chain(v.tensor_reduce(tmp[:], prod, AX.X, ALU.add))
            chain(v.tensor_tensor(bq[:], bq[:], tmp[:], ALU.add))
            chain(v.tensor_tensor(wn, wn, gwb, ALU.mult))
            chain(v.tensor_reduce(bound[:], wn, AX.X, ALU.add, apply_absolute_value=True))
            chain(v.tensor_scalar(tmp[:], bq[:], -1.0, None, ALU.mult))
            chain(v.tensor_tensor(tmp[:], tmp[:], bq[:], ALU.max))
            chain(v.scalar_tensor_tensor(bound[:], bound[:], XS, tmp[:], ALU.mult, ALU.add))
            chain(v.tensor_scalar(bound[:], bound[:], 1e-30, None, ALU.max))
            chain(v.memset(ones, 1.0))
            dve.wait_ge(consts, 3)
            for p in range(PAIRS):
                last = v.tensor_scalar(diag[:, p, :], id32[:], bound[:, 8 + p:9 + p], None, ALU.mult)
            last.then_inc(setup_dve, 1)
            chain(v.reciprocal(omega[:], bound[:]))
            chain(v.tensor_scalar(omega[:], omega[:], ROW * XS, None, ALU.mult))
            v.tensor_tensor(wn, wn, omega[:].unsqueeze(2).to_broadcast([P, 12, C]), ALU.mult) \
                .then_inc(setup_dve, 1)
            chain(v.tensor_reduce(top2[:], bound[:, 0:8].rearrange("p (k m) -> p k m", k=2), AX.X, ALU.max))
            dve.sem_inc(setup_pool, 1)
            dve.wait_ge(setup_pool, 2)
            chain(v.tensor_tensor(sscale[:], gtop[:, 0:1], gtop[:, 1:2], ALU.mult))
            chain(v.tensor_scalar(sscale[:], sscale[:], float(D) ** -0.5 / TOP ** 2, None, ALU.mult))
            chain(v.reciprocal(top2[:], gtop[:]))
            chain(v.tensor_scalar(top2[:], top2[:], TOP, None, ALU.mult))
            for k in range(2):
                m = slice(4 * k, 4 * k + 4)
                chain(v.tensor_scalar(cq[:, m], bound[:, m], top2[:, k:k + 1], 1.0 / (XS * ROW * XS),
                                      ALU.mult, ALU.mult))
                chain(v.tensor_scalar(bq[:, m], bq[:, m], top2[:, k:k + 1], None, ALU.mult))
            chain(v.tensor_scalar(tmp[:, 8:12], omega[:, 8:12], TOP / (ROW * XS), None, ALU.mult))
            chain(v.tensor_tensor(bq[:, 8:12], bq[:, 8:12], tmp[:, 8:12], ALU.mult))
            dve.wait_ge(setup_pe, 1)
            brow = AV[:].rearrange("p a t -> p (a t)").unsqueeze(1).to_broadcast([P, 4, C])
            chain(v.tensor_tensor(wpn, wpn, brow, ALU.mult))
            chain(v.tensor_reduce(cp[:], wpn, AX.X, ALU.add, apply_absolute_value=True))
            chain(v.tensor_scalar(cp[:], cp[:], 1e-30, None, ALU.max))
            chain(v.reciprocal(tmp[:, 0:4], cp[:]))
            chain(v.tensor_scalar(tmp[:, 0:4], tmp[:, 0:4], ROW, None, ALU.mult))
            chain(v.tensor_scalar(cp[:], cp[:], 1.0 / (ROW * TOP), None, ALU.mult))
            v.tensor_tensor(wpn, wpn, tmp[:, 0:4].unsqueeze(2).to_broadcast([P, 4, C]), ALU.mult) \
                .then_inc(setup_dve, 1)
            for m in range(16):
                dve.wait_ge(w_hi, m + 1)
                cols = slice(m * P, m * P + P) if m < 12 else slice((m - 12) * P, (m - 11) * P)
                W = Wqkv if m < 12 else Wp
                v.tensor_tensor(W[:, LO, :, cols], wbank[:, m % 4], W[:, HI, :, cols], ALU.subtract) \
                    .then_inc(w_lo, 1)

            def group_mean(X, r):
                dve.wait_ge(stat_out, X * 4 + (2 * r + 1))
                wait(dve, xy_done, X * 4 + 2 * r)
                v.tensor_scalar(ngm[:], FB[:, 0:2], -1.0, None, ALU.mult).then_inc(stat_read, 1)

            def group_variance(X, r):
                dve.wait_ge(stat_out, X * 4 + (2 * r + 2))
                v.tensor_scalar(na[:], FB[:, 0:2], EPS, None, ALU.add).then_inc(stat_read, 1)
                dve.wait_ge(stat_read, X * 4 + (2 * r + 2))
                v.tensor_scalar(hv[:], na[:], -0.5, None, ALU.mult)
                chain(v.tensor_scalar(ny[:].bitcast(U32), na[:].bitcast(U32), 1, None,
                                      ALU.logical_shift_right))
                v.tensor_scalar(ny[:].bitcast(U32), ny[:].bitcast(U32), -1.0, 1597463007.0,
                                ALU.mult, ALU.add).then_inc(guessed, 1)

            def scaled_filler(F, item):
                kind, i0, i1 = item
                dve.wait_ge(filler_psum, F + 1)
                wait(dve, filler_out, F)
                if kind == "v":
                    ins = v.tensor_scalar(yf[:], FB[:], TOP / (XS * ROW * XS), None, ALU.mult)
                elif kind == "qk":
                    m = (i1 // 2) * 4 + i0
                    ins = v.tensor_scalar(yf[:], FB[:], cq[:, m:m + 1], bq[:, m:m + 1], ALU.mult, ALU.add)
                else:
                    ins = v.tensor_scalar(yf[:], FB[:], cp[:, i1:i1 + 1], bp[:, i1:i1 + 1], ALU.mult, ALU.add)
                ins.then_inc(y_done, 1)

            def row_max(b, i):
                dve.wait_ge(s_done, b * STEPS + (i + 1))
                q = i % 4
                chain(v.tensor_reduce(nmax[:, q:q + 1], SC[:, i % 2, :], AX.X, ALU.max, negate=True))
                v.tensor_scalar(nbias[:, q:q + 1], nmax[:, q:q + 1], sscale[:, 0:1], None, ALU.mult) \
                    .then_inc(nb_done, 1)

            def normalised_outputs(count):
                dve.wait_ge(r_copied, count + 1)
                wait(dve, at_done, count)
                v.scalar_tensor_tensor(at[:], AV[:, 0, :], 1.0 / (PS * RS), rsb[:], ALU.mult, ALU.mult) \
                    .then_inc(av_read, 1)

            def outputs_lo(count, g):
                pair, u = g // 4, g % 4
                cols = slice(u * TG, (u + 1) * TG)
                dve.wait_ge(ah_done, count + 1)
                v.scalar_tensor_tensor(AT[:, LO, pair, cols], at[:], bq[:, 8 + pair:9 + pair],
                                       AT[:, HI, pair, cols], ALU.add, ALU.subtract).then_inc(at_done, 1)

            def normalised(X, r, c):
                dve.wait_ge(norm_ready, X * 2 + (r + 1))
                v.tensor_scalar(xc[:, c, :], xc[:, c, :], ngm[:, c:c + 1], rs[:, c:c + 1],
                                ALU.add, ALU.mult).then_inc(xy_done, 1)

            def reciprocals(count, gpar):
                dve.wait_ge(e_done, (count + 1) * 4)
                wait(dve, rb_done, count - 1)
                v.reciprocal(rinv[:, gpar, :], acc[:, gpar, :]).then_inc(ri_done, 1)

            for r in range(2):
                group_mean(0, r)
                group_variance(0, r)
                for c in range(2):
                    normalised(0, r, c)
            for F, item in enumerate(HEAD_START):
                scaled_filler(F, item)
            row_max(0, 0)

            def batch(b, par, first, last):
                slots = slots_of(b, first, last)
                for i in range(STEPS):
                    g, k, a, j = i // 4, i % 4, i % 2, (i % 4) // 2
                    if i + 1 < STEPS:
                        row_max(b, i + 1)
                    elif not last:
                        row_max(b + 1, 0)
                    if i % 2 == 1 and i // 2 in slots:
                        scaled_filler(filler_number(b, i // 2), slots[i // 2][0])
                    if k == 0:
                        if not (first and g < 2):
                            normalised_outputs(b * 16 + (g - 2))
                        if not (first and g < 1):
                            reciprocals(b * 16 + (g - 1), (g - 1) % 2)
                    dve.wait_ge(ph_done, b * STEPS + (i + 1))
                    v.scalar_tensor_tensor(PT[:, g % 2, a, LO, :, j * P:(j + 1) * P], TP[:], PS,
                                           PT[:, g % 2, a, HI, :, j * P:(j + 1) * P],
                                           ALU.mult, ALU.subtract).then_inc(pl_done, 1)
                    if k == 0 and not (first and g < 2):
                        outputs_lo(b * 16 + (g - 2), (g - 2) % 16)
                    if not last:
                        for r in range(2):
                            if i == MEAN_STEP[r]:
                                group_mean(b + 1, r)
                            if i == VAR_STEP[r]:
                                group_variance(b + 1, r)
                            if 0 <= i - NORM_STEP[r] < 2:
                                normalised(b + 1, r, i - NORM_STEP[r])

            run_batches(dve, batch, chain)
            normalised_outputs(16 * B - 2)
            reciprocals(16 * B - 1, 1)
            outputs_lo(16 * B - 2, 14)
            normalised_outputs(16 * B - 1)
            outputs_lo(16 * B - 1, 15)
            for s in range(8):
                scaled_filler(filler_number(B - 1, AHEAD + s), SLOTS[s])

        @block.gpsimd
        def _(pool):
            v = nc.gpsimd
            chain = Chain(pool, pool_chain)
            chain.per_batch = POOL_CHAIN
            chain(v.memset(id32[:], 0.0))
            v.affine_select(out=id32[:], in_=id32[:], compare_op=ALU.not_equal, fill=1.0, base=0,
                            pattern=[[-1, P]], channel_multiplier=1).then_inc(consts, 1)
            chain(v.memset(id16[:], 0.0))
            v.affine_select(out=id16[:], in_=id16[:], compare_op=ALU.not_equal, fill=1.0, base=0,
                            pattern=[[-1, P]], channel_multiplier=1).then_inc(consts, 1)
            chain(v.memset(gavg[:], 1.0 / (CPG * T)))
            gv = gavg[:].rearrange("p (g c) -> p g c", c=CPG)
            chain(v.affine_select(out=gv, in_=gv, compare_op=ALU.is_ge, fill=0.0, base=0,
                                  pattern=[[-CPG, P // CPG], [0, CPG]], channel_multiplier=1))
            v.affine_select(out=gv, in_=gv, compare_op=ALU.is_ge, fill=0.0, base=CPG - 1,
                            pattern=[[CPG, P // CPG], [0, CPG]], channel_multiplier=-1).then_inc(consts, 1)
            chain.alone = True
            pool.wait_ge(setup_pool, 1)
            v.partition_all_reduce(gtop[:], top2[:], P, RMAX).then_inc(setup_pool, 1)

            def inverse_std(X, r):
                apart(pool, X * 2 + (r + 1), X * 4 + 2 * r)
                pool.wait_ge(guessed, X * 2 + (r + 1))
                wait(pool, xy_done, X * 4 + 2 * r)
                for _ in range(4):
                    chain.alone = False
                    chain(v.tensor_tensor(na[:], ny[:], ny[:], ALU.mult))
                    chain.alone = True
                    chain(v.tensor_tensor(na[:], na[:], hv[:], ALU.mult))
                    chain.alone = False
                    chain(v.tensor_scalar(na[:], na[:], 1.5, None, ALU.add))
                    chain.alone = True
                    chain(v.tensor_tensor(ny[:], na[:], ny[:], ALU.mult))
                v.tensor_scalar(rs[:], ny[:], XS, None, ALU.mult).then_inc(norm_ready, 1)

            def normalised_lo(X, par, r, c):
                kc = 2 * r + c
                pool.wait_ge(xh_done, X * 4 + (kc + 1))
                v.tensor_tensor(XN[:, par, LO, kc, :], xc[:, c, :], XN[:, par, HI, kc, :],
                                ALU.subtract).then_inc(xn_done, 1)

            def use_filler(F, item, b, par, parts):
                kind, i0, i1 = item
                if kind == "proj":
                    i = 4 * i0 + i1
                    pool.wait_ge(y_done, F + 1)
                    pool.wait_ge(res_loaded[i % 2], b * 64 + 16 * (i // 2 + 1))
                    ins = v.tensor_tensor(xres[:, i % 2, :], xres[:, i % 2, :], yf[:], ALU.add)
                else:
                    hi, lo = ((V[:, par, HI, i0, :], V[:, par, LO, i0, :]) if kind == "v" else
                              (nat[:, i1 % 2, HI, :], nat[:, i1 % 2, LO, :]))
                    pool.wait_ge(yh_done, parts)
                    ins = v.tensor_tensor(lo, yf[:], hi, ALU.subtract)
                ins.then_inc(filler_out, 1)

            def reciprocal_parts(count, gpar):
                apart(pool, count + 1, count)
                pool.wait_ge(ri_done, count + 1)
                wait(pool, av_done, count)
                chain(v.tensor_scalar(rscl[:], rinv[:, gpar, :], RS, None, ALU.mult))
                wide = rscl[:].unsqueeze(2).to_broadcast([P, 4, D])
                chain(v.tensor_copy(rb[:, HI], wide))
                v.tensor_tensor(rb[:, LO], wide, rb[:, HI], ALU.subtract).then_inc(rb_done, 1)

            for r in range(2):
                inverse_std(0, r)
                for c in range(2):
                    normalised_lo(0, 0, r, c)
            for F, item in enumerate(HEAD_START):
                use_filler(F, item, 0, 0, F + 1)

            def batch(b, par, first, last):
                slots = slots_of(b, first, last)
                for i in range(STEPS):
                    g, k = i // 4, i % 4
                    if i % 2 == 1 and i // 2 in slots:
                        item, off = slots[i // 2]
                        use_filler(filler_number(b, i // 2), item, b + off, (par + off) % 2,
                                   b * 24 + (i // 2 + 9))
                    if k == 0 and not (first and g < 1):
                        reciprocal_parts(b * 16 + (g - 1), (g - 1) % 2)
                    for r in range(2):
                        if i == RSQRT_STEP[r] and not last:
                            inverse_std(b + 1, r)
                        for c in range(2):
                            if i == PARTS_STEP[r] + c and not last:
                                normalised_lo(b + 1, 1 - par, r, c)

            run_batches(pool, batch, chain)
            reciprocal_parts(16 * B - 1, 1)
            for s in range(8):
                use_filler(filler_number(B - 1, AHEAD + s), SLOTS[s], B - 1, 1, None)


DVE_CHAIN = 66
POOL_CHAIN = 64

_INS = ["x", "L0_conv_gn_w", "L0_conv_gn_b", "L0_conv_qkv_w", "L0_conv_qkv_b", "L0_conv_proj_w", "L0_conv_proj_b"]


def kernel(**inputs):
    import numpy as _np
    import concourse.bacc as _bacc
    from concourse import mybir as _mybir
    from concourse.bass_utils import run_bass_kernel_spmd as _run

    nc = _bacc.Bacc("TRN2", target_bir_lowering=False, num_devices=1)
    arrays, args = {}, []
    for name in _INS:
        a = _np.ascontiguousarray(inputs[name])
        arrays[f"in_{name}_dram"] = a
        args.append(nc.dram_tensor(f"in_{name}_dram", a.shape, _mybir.dt.from_np(a.dtype), kind="ExternalInput").ap())
    shape = inputs["x"].shape
    args.append(nc.dram_tensor("out_dram", shape, _mybir.dt.from_np(_np.dtype("float32")), kind="ExternalOutput").ap())
    bass_groupnorm_attention_kernel(nc, *args)
    r = _run(nc, [arrays], core_ids=[0])
    return r.results[0]["out_dram"]
```

```python
from contextlib import ExitStack

import concourse.bass as bass
from concourse import mybir

F32 = mybir.dt.float32
F16 = mybir.dt.float16
U32 = mybir.dt.uint32
ALU = mybir.AluOpType
ACT = mybir.ActivationFunctionType
AX = mybir.AxisListType
RMAX = bass.bass_isa.ReduceOp.max

P = 128
HEADS = 8
GROUPS = 32
EPS = 1e-5
HI, LO = 0, 1

XS = 2.0 ** 7
ROW = 2.0 ** 14
TOP = 2.0 ** 15
PS = 2.0 ** 14

SLOTS = ([("proj", n, m) for n in range(2) for m in range(4)]
         + [("qk", 2, n) for n in range(4)] + [("qk", 3, n) for n in range(4)]
         + [("v", s, 0) for s in range(8)]
         + [("qk", 0, n) for n in range(4)] + [("qk", 1, n) for n in range(4)])
AHEAD = 16
HEAD_START = SLOTS[AHEAD + 8:AHEAD + 12] + SLOTS[AHEAD:AHEAD + 8]
FIRST_SLOTS = SLOTS[AHEAD + 12:]
W_ORDER = [8, 9, 10, 11, 4, 5, 6, 7, 0, 1, 2, 3]
STACK = [0, 1, 0, 2]

SUM_STEPS = [2, 3, 4, 6]
MEAN_STEP = 7
SQUARE_STEPS = [8, 10, 11, 12]
VAR_STEP = 15
RSQRT_STEP = 16
NORM_STEPS = [18, 20, 22, 24]
PARTS_STEPS = [20, 22, 24, 28]


def filler_number(b, slot):
    if isinstance(b, int) and b == 0 and slot < 8:
        return 12 + slot
    return b * 32 + 8 + slot


def bass_groupnorm_attention_kernel(nc, x, gn_w, gn_b, qkv_w, qkv_b, proj_w, proj_b, out):
    B, C, HH, WW = x.shape
    T = HH * WW
    D = C // HEADS
    KC = C // P
    PAIRS = HEADS // 2
    ST = T // P
    STEPS = HEADS * ST
    TG = 2 * P
    CPG = C // GROUPS
    assert (C, T, D, KC, STEPS, CPG) == (512, 1024, 64, 4, 64, 16) and B % 2 == 0
    assert CPG * T == 2 ** 14

    xr_v = x.rearrange("b c h w -> b c (h w)")
    out_v = out.rearrange("b c h w -> b c (h w)")

    with ExitStack() as ctx:
        def sb(name, shape, dt):
            return ctx.enter_context(nc.sbuf_tensor(name, shape, dt))

        def sem(name):
            return ctx.enter_context(nc.semaphore(name))

        Wqkv = sb("Wqkv", [P, 2, KC, 3 * C], F16)
        Wp = sb("Wp", [P, 2, KC, C], F16)
        XN = sb("XN", [P, 2, 2, KC, T], F16)
        xc = sb("xc", [P, KC, T], F32)
        V = sb("V", [P, 2, 2, ST, C], F16)
        PT = sb("PT", [P, 2, 2, ST, P], F16)
        Pr = sb("Pr", [P, 2, T], F32)
        yf = sb("yf", [P, 512], F32)
        nat = sb("nat", [P, 2, 2, 512], F16)
        QK = sb("QK", [P, 3, 3, 2, T], F16)
        QS, KH, KL = QK[:, 0], QK[:, 1], QK[:, 2]
        AT = sb("AT", [P, 2, KC, T], F16)
        on = sb("on", [P, 4, D], F32)
        at = sb("at", [P, TG], F32)
        xres = sb("xres", [P, 8, 512], F32)
        id32 = sb("id32", [P, P], F32)
        gavg = sb("gavg", [P, P], F32)
        acc = sb("acc", [P, 2, 4], F32)
        rinv = sb("rinv", [P, 2, 4], F32)
        nmax = sb("nmax", [P, 4], F32)
        nbias = sb("nbias", [P, 4], F32)
        sscale = sb("sscale", [P, 1], F32)
        cq = sb("cq", [P, 12], F32)
        bq = sb("bq", [P, 12], F32)
        cp = sb("cp", [P, 4], F32)
        bp = sb("bp", [P, 4], F32)
        sums = sb("sums", [P, 2, KC], F32)
        ngm = sb("ngm", [P, KC], F32)
        rs = sb("rs", [P, KC], F32)
        hv = sb("hv", [P, KC], F32)
        ny = sb("ny", [P, KC], F32)
        na = sb("na", [P, KC], F32)
        bound = sb("bound", [P, 12], F32)
        dots = sb("dots", [P, 12], F32)
        tmp = sb("tmp", [P, 12], F32)
        omega = sb("omega", [P, 12], F32)
        top2 = sb("top2", [P, 2], F32)
        gtop = sb("gtop", [P, 2], F32)

        borrowed = QK[:].rearrange("p a b c d -> p (a b c d)").bitcast(F32)
        wn = borrowed[:, 0:12 * C].rearrange("p (m c) -> p m c", c=C)
        wpn = PT[:].rearrange("p a b c t -> p (a b c t)").bitcast(F32).rearrange("p (m c) -> p m c", c=C)
        borrowed_v = V[:].rearrange("p a b c d -> p (a b c d)").bitcast(F32)
        prod = borrowed_v[:, 0:12 * C].rearrange("p (m c) -> p m c", c=C)
        gw = borrowed_v[:, 12 * C:13 * C]
        gb = borrowed_v[:, 13 * C:14 * C]
        diag = borrowed_v[:, 14 * C:15 * C].rearrange("p (m c) -> p m c", c=P)
        ones = borrowed_v[:, 15 * C:15 * C + P]
        unused = AT[:].rearrange("p a b t -> p (a b t)").rearrange("p (n c) -> p n c", c=512)

        SC = ctx.enter_context(nc.psum_tensor("SC", [P, 2, T], F32))
        TP = ctx.enter_context(nc.psum_tensor("TP", [P, ST, P], F32))
        AV = ctx.enter_context(nc.psum_tensor("AV", [P, 2, TG], F32))
        FB = ctx.enter_context(nc.psum_tensor("FB", [P, 512], F32))
        TPB = TP[:, 0:4, :].rearrange("p c t -> p (c t)")
        wbank = SC[:].rearrange("p a (b m c) -> p (a b) m c", b=2, c=P)

        gn_loaded = sem("gn_loaded")
        w_loaded = [sem(f"w_loaded{c}") for c in range(3)]
        bias_loaded = sem("bias_loaded")
        wp_loaded = sem("wp_loaded")
        consts = sem("consts")
        w_times_gn = sem("w_times_gn")
        w_summed = sem("w_summed")
        w_scaled = sem("w_scaled")
        tops = sem("tops")
        v_bounds = sem("v_bounds")
        v_bounds_wide = sem("v_bounds_wide")
        wp_scaled = sem("wp_scaled")
        w_turned = sem("w_turned")
        w_hi = sem("w_hi")
        w_lo = sem("w_lo")
        xc_loaded = [sem(f"xc_loaded{c}") for c in range(KC)]
        res_loaded = [sem(f"res_loaded{c}") for c in range(8)]
        stored = [sem(f"stored{c}") for c in range(8)]
        stacked = [sem(f"stacked{c}") for c in range(2)]
        stat_in = sem("stat_in")
        stat_out = sem("stat_out")
        stat_read = sem("stat_read")
        guessed = sem("guessed")
        norm_ready = sem("norm_ready")
        xy_done = sem("xy_done")
        xn_done = sem("xn_done")
        s_done = sem("s_done")
        nb_done = sem("nb_done")
        e_done = sem("e_done")
        t_done = sem("t_done")
        ph_done = sem("ph_done")
        xh_done = sem("xh_done")
        yh_done = sem("yh_done")
        pl_done = sem("pl_done")
        ri_done = sem("ri_done")
        av_done = sem("av_done")
        on_done = sem("on_done")
        ot_done = sem("ot_done")
        at_read = sem("at_read")
        at_done = sem("at_done")
        filler_psum = sem("filler_psum")
        y_done = sem("y_done")
        filler_out = sem("filler_out")
        dve_chain = sem("dve_chain")
        pool_chain = sem("pool_chain")

        block = ctx.enter_context(nc.Block())

        def wait(eng, s, value):
            if not isinstance(value, int) or value > 0:
                eng.wait_ge(s, value)

        def apart(eng, *values):
            for value in values:
                if not isinstance(value, int):
                    eng.compute_val(value)
            eng.wait_ge(consts, 2)

        class Chain:

            def __init__(self, eng, s):
                self.eng, self.sem, self.base, self.n, self.alone = eng, s, 0, 0, False

            def __call__(self, ins):
                self.n += 1
                ins.then_inc(self.sem, 1)
                if self.alone:
                    apart(self.eng, self.base + self.n)
                self.eng.wait_ge(self.sem, self.base + self.n)

        def run_batches(eng, batch, chain=None):
            batch(0, 0, True, False)
            if chain:
                before = chain.n
            with eng.Fori(0, B // 2 - 1) as j:
                if chain:
                    chain.base, chain.n = before + j * (2 * chain.per_batch), 0
                batch(j * 2 + 1, 1, False, False)
                batch(j * 2 + 2, 0, False, False)
                if chain:
                    assert chain.n == 2 * chain.per_batch, (chain.n, chain.per_batch)
            if chain:
                chain.base, chain.n = 0, before + (B - 2) * chain.per_batch
            batch(B - 1, 1, False, True)

        def slots_of(b, first, last):
            found = {}
            for s, item in enumerate(SLOTS):
                if first and s < 4:
                    found[s] = (FIRST_SLOTS[s], 0)
                if first and s < 8 or last and s >= AHEAD:
                    continue
                found[s] = (item, -1 if item[0] == "proj" else 1 if s >= AHEAD else 0)
            return found

        @block.sync
        def _(sp):
            sp.dma_start(gw, gn_w.partition_broadcast(P)).then_inc(gn_loaded, 16)
            sp.dma_start(gb, gn_b.partition_broadcast(P)).then_inc(gn_loaded, 16)
            w_rows = qkv_w.rearrange("(q a k r) c -> a k r q c", a=2, k=3, r=D)
            b_rows = qkv_b.rearrange("(q a k r) -> a k r q", a=2, k=3, r=D)
            for kind in (2, 1, 0):
                for a in range(2):
                    sp.dma_start(wn[a * D:(a + 1) * D, kind * 4:kind * 4 + 4, :], w_rows[a, kind]) \
                        .then_inc(w_loaded[kind], 16)
            for kc in range(KC):
                sp.dma_start(xc[:, kc, :], xr_v[0, kc * P:(kc + 1) * P, :]).then_inc(xc_loaded[kc], 16)
            for kind in range(3):
                for a in range(2):
                    sp.dma_start(bq[a * D:(a + 1) * D, kind * 4:kind * 4 + 4], b_rows[a, kind],
                                 allow_slow_non_contiguous=True).then_inc(bias_loaded, 16)
            sp.dma_start(bp[:], proj_b.rearrange("(m p) -> p m", p=P), allow_slow_non_contiguous=True) \
                .then_inc(bias_loaded, 16)
            sp.dma_start(wpn, proj_w.rearrange("(m p) c -> p m c", p=P)).then_inc(wp_loaded, 16)

            def load_chunks(X):
                for kc in range(KC):
                    apart(sp, X * 4 + (kc - 3))
                    wait(sp, xn_done, X * 4 + (kc - 3))
                    sp.dma_start(xc[:, kc, :], xr_v[X, kc * P:(kc + 1) * P, :]).then_inc(xc_loaded[kc], 16)

            def load_residual(b, i):
                n, m = i // 4, i % 4
                apart(sp, b * 16)
                wait(sp, stored[i], b * 16)
                sp.dma_start(xres[:, i, :], xr_v[b, m * P:(m + 1) * P, n * 512:(n + 1) * 512]) \
                    .then_inc(res_loaded[i], 16)

            def store(b, i, F):
                n, m = i // 4, i % 4
                apart(sp, F + 1)
                sp.wait_ge(filler_out, F + 1)
                sp.dma_start(out_v[b, m * P:(m + 1) * P, n * 512:(n + 1) * 512], xres[:, i, :]) \
                    .then_inc(stored[i], 16)

            def stack_qk(b, pair, n, F):
                kind, half = n // 2, n % 2
                cols = slice(half * 512, half * 512 + 512)
                buf = STACK[pair]
                scored = b * STEPS + [-16, -32, 16, 0][pair]
                apart(sp, F + 1, scored)
                sp.wait_ge(filler_out, F + 1)
                wait(sp, s_done, scored)
                for a in range(2):
                    rows = slice(a * D, a * D + D)
                    if kind == 0:
                        for part in (HI, LO):
                            sp.dma_start(QS[part * D:part * D + D, buf, a, cols], nat[rows, half, part, :]) \
                                .then_inc(stacked[half], 16)
                    else:
                        for part, dst in ((HI, KH), (LO, KL)):
                            for z in range(2):
                                sp.dma_start(dst[z * D:z * D + D, buf, a, cols], nat[rows, half, part, :]) \
                                    .then_inc(stacked[half], 16)

            for F, item in enumerate(HEAD_START):
                if item[0] == "qk":
                    stack_qk(0, item[1], item[2], F)

            def batch(b, par, first, last):
                if not last:
                    load_chunks(b + 1)
                for s, (item, off) in slots_of(b, first, last).items():
                    F = filler_number(b, s)
                    if item[0] == "proj":
                        store(b - 1, s, F)
                    if 8 <= s < 16:
                        load_residual(b, s - 8)
                    if item[0] == "qk":
                        stack_qk(b + off, item[1], item[2], F)

            run_batches(sp, batch)
            for s in range(8):
                store(B - 1, s, filler_number(B - 1, AHEAD + s))
            for s in range(8):
                sp.wait_ge(stored[s], B * 16)

        @block.tensor
        def _(pe):
            def w_transposes(n):
                if n >= 4:
                    pe.wait_ge(w_lo, n - 3)
                if n < 12:
                    pe.wait_ge(w_scaled, n + 1)
                    src = wn[:, W_ORDER[n], :]
                else:
                    pe.wait_ge(wp_scaled, 1)
                    src = wpn[:, n - 12, :]
                for kc in range(KC):
                    last = nc.tensor.transpose(wbank[:, n % 4, kc, :], src[:, kc * P:(kc + 1) * P], id32[:])
                last.then_inc(w_turned, 1)

            def filler(F, item, b, par, part_of, bank=FB[:], read=None):
                kind, i0, i1 = item
                if part_of == 0:
                    wait(pe, y_done, F if read is None else read)
                    if kind == "proj" and i1 == 0:
                        pe.wait_ge(at_done, b * 16 + (14 if i0 == 0 else 16))
                for kc in (0, 1) if part_of == 0 else (2, 3):
                    if isinstance(F, int) and F == 0 or kind == "v" and i0 == 0:
                        pe.wait_ge(xn_done, b * 4 + (kc + 1))
                    for ps, pm in ((HI, HI), (HI, LO), (LO, HI)):
                        if kind == "qk":
                            m = (i1 // 2) * 4 + i0
                            lhsT = Wqkv[:, ps, kc, m * P:(m + 1) * P]
                            rhs = XN[:, par, pm, kc, (i1 % 2) * 512:(i1 % 2) * 512 + 512]
                        elif kind == "v":
                            lhsT = XN[:, par, ps, kc, i0 * P:(i0 + 1) * P]
                            rhs = Wqkv[:, pm, kc, 2 * C:3 * C]
                        else:
                            lhsT = Wp[:, ps, kc, i1 * P:(i1 + 1) * P]
                            rhs = AT[:, pm, kc, i0 * 512:i0 * 512 + 512]
                        last = nc.tensor.matmul(bank, lhsT, rhs, start=(kc == 0 and ps == pm),
                                                stop=(kc == 3 and ps == LO))
                if part_of == 1:
                    last.then_inc(filler_psum, 1)

            def group_average(X, stage):
                pe.wait_ge(stat_in, X * 2 + (stage + 1))
                nc.tensor.matmul(AV[:, 1, 0:KC], gavg[:], sums[:, stage, :], start=True, stop=True) \
                    .then_inc(stat_out, 1)

            def scores(b, i, first_tile):
                pair, u, j, a = i // 16, (i // 4) % 4, (i % 4) // 2, i % 2
                t0 = (2 * u + j) * P
                if i % 16 == 0:
                    for half in range(2):
                        pe.wait_ge(stacked[half], b * (192 * PAIRS) + 192 * (pair + 1))
                if not (first_tile and i < 2):
                    pe.wait_ge(e_done, b * STEPS + (i - 1))
                for half in range(2):
                    for K, start in ((KH, True), (KL, False)):
                        last = nc.tensor.matmul(SC[:, i % 2, half * 512:half * 512 + 512],
                                                QS[:, STACK[pair], a, t0:t0 + P],
                                                K[:, STACK[pair], a, half * 512:half * 512 + 512],
                                                start=start, stop=not start)
                last.then_inc(s_done, 1)

            def transposes(b, i):
                pe.wait_ge(e_done, b * STEPS + (i + 1))
                for half in range(2):
                    wait(pe, pl_done, b * (2 * STEPS) + (2 * i - 1 + half))
                    for c in range(4 * half, 4 * half + 4):
                        last = nc.tensor.transpose(TP[:, c, :], Pr[:, i % 2, c * P:(c + 1) * P], id32[:])
                    last.then_inc(t_done, 1)

            def weighted_sum(b, i, par):
                h = 2 * (i // 16) + i % 2
                if i == 0:
                    pe.wait_ge(filler_out, 12 if isinstance(b, int) and b == 0 else b * 32)
                if i % 4 == 0:
                    wait(pe, on_done, b * 16 + i // 4)
                if i % 4 == 1:
                    wait(pe, at_read, b * 16 + i // 4)
                for c in range(ST):
                    for pp, pv in ((HI, HI), (HI, LO), (LO, HI)):
                        last = nc.tensor.matmul(AV[:, 0, (i % 4) * D:(i % 4) * D + D], PT[:, i % 2, pp, c, :],
                                                V[:, par, pv, c, h * D:(h + 1) * D],
                                                start=(c == 0 and pp == pv), stop=(c == ST - 1 and pp == LO))
                if i % 4 == 3:
                    last.then_inc(av_done, 1)

            def outputs_transposed(count):
                pe.wait_ge(on_done, count + 1)
                for j in range(2):
                    last = nc.tensor.transpose(AV[:, 1, j * P:(j + 1) * P],
                                               on[:, 2 * j:2 * j + 2, :].rearrange("p a d -> p (a d)"), id32[:])
                last.then_inc(ot_done, 1)

            pe.wait_ge(consts, 2)
            for n in range(4):
                w_transposes(n)
            group_average(0, 0)
            for n in range(4, 6):
                w_transposes(n)
            pe.wait_ge(stat_read, 1)
            group_average(0, 1)
            for n in range(6, 12):
                w_transposes(n)
            for F, item in enumerate(HEAD_START):
                for part_of in range(2):
                    filler(F, item, 0, 0, part_of, TPB if F % 2 else FB[:], F - 1)
                if F == 0:
                    pe.wait_ge(stat_read, 2)
                    pe.wait_ge(v_bounds, 1)
                    nc.tensor.matmul(AV[:].rearrange("p a t -> p (a t)"), ones,
                                     diag.rearrange("p m c -> p (m c)"), start=True, stop=True) \
                        .then_inc(v_bounds_wide, 1)
                if F == 5:
                    for n in range(12, 16):
                        w_transposes(n)
            scores(0, 0, True)

            def batch(b, par, first, last):
                slots = slots_of(b, first, last)
                for i in range(STEPS):
                    if i + 1 < STEPS:
                        scores(b, i + 1, first)
                    elif not last:
                        scores(b + 1, 0, False)
                    s = i // 2
                    if s in slots:
                        item, off = slots[s]
                        filler(filler_number(b, s), item, b + off, (par + off) % 2, i % 2)
                    transposes(b, i)
                    if i - 1 in (MEAN_STEP, VAR_STEP) and not last:
                        pe.wait_ge(stat_read, b * 2 + (3 if i - 1 == MEAN_STEP else 4))
                    if i > 0:
                        weighted_sum(b, i - 1, par)
                    elif not first:
                        weighted_sum(b - 1, STEPS - 1, 1 - par)
                    if i % 4 == 1 and not (first and i < 4):
                        outputs_transposed(b * 16 + (i // 4 - 1))
                    if i in (MEAN_STEP, VAR_STEP) and not last:
                        group_average(b + 1, (i == VAR_STEP) * 1)

            run_batches(pe, batch)
            pe.wait_ge(pl_done, 2 * B * STEPS)
            weighted_sum(B - 1, STEPS - 1, 1)
            outputs_transposed(B * 16 - 1)
            for s in range(8):
                F = filler_number(B - 1, AHEAD + s)
                for part_of in range(2):
                    filler(F, SLOTS[s], B - 1, 1, part_of, TPB if s % 2 else FB[:], F - 1 if s else F)

        @block.scalar
        def _(act):
            def w_parts_hi(n):
                act.wait_ge(w_turned, n + 1)
                m = W_ORDER[n] if n < 12 else n - 12
                dst = (Wqkv if n < 12 else Wp)[:, HI, :, m * P:(m + 1) * P]
                nc.scalar.activation(dst, wbank[:, n % 4], ACT.Copy).then_inc(w_hi, 1)

            def numerators(b, i):
                act.wait_ge(nb_done, b * STEPS + (i + 1))
                wait(act, t_done, b * (2 * STEPS) + (2 * i - 2))
                nc.scalar.activation(Pr[:, i % 2], SC[:, i % 2, :], ACT.Exp, bias=nbias[:, i % 4:i % 4 + 1],
                                     scale=sscale[:, 0:1],
                                     accum_out=acc[:, (i // 4) % 2, i % 4:i % 4 + 1]).then_inc(e_done, 1)

            def outputs_read(count, pair):
                act.wait_ge(ot_done, count + 1)
                wait(act, at_done, count)
                nc.scalar.activation(at[:], AV[:, 1, :], ACT.Identity, bias=bq[:, 8 + pair:9 + pair]) \
                    .then_inc(at_read, 1)

            def sum_pass(X, par, stage, kc):
                if stage == 0:
                    act.wait_ge(xc_loaded[kc], X * 16 + 16)
                    if kc == 0:
                        wait(act, filler_psum, (X - 2) * 32 + 24)
                elif kc == 0:
                    act.wait_ge(stat_read, X * 2 + 1)
                ins = nc.scalar.activation(XN[:, par, HI, kc, :], xc[:, kc, :],
                                           ACT.Square if stage else ACT.Identity,
                                           bias=ngm[:, kc:kc + 1] if stage else 0.0,
                                           accum_out=sums[:, stage, kc:kc + 1])
                if kc == KC - 1:
                    ins.then_inc(stat_in, 1)

            def normalised_hi(X, par, kc):
                act.wait_ge(xy_done, X * 4 + (kc + 1))
                nc.scalar.activation(XN[:, par, HI, kc, :], xc[:, kc, :], ACT.Copy).then_inc(xh_done, 1)

            def filler_hi(F, item, b, par):
                kind, i0, i1 = item
                if kind == "proj":
                    return
                act.wait_ge(y_done, F + 1)
                if kind == "v":
                    hi = V[:, par, HI, i0, :]
                    if i0 == 0:
                        wait(act, av_done, (b - 1) * 16)
                else:
                    half = i1 % 2
                    hi = nat[:, half, HI, :]
                    wait(act, stacked[half], b * (192 * PAIRS) + (192 * i0 + (64 if i1 >= 2 else 0)))
                nc.scalar.activation(hi, yf[:], ACT.Copy).then_inc(yh_done, 1)

            for n, m in enumerate(W_ORDER):
                act.wait_ge(w_times_gn, n + 1)
                nc.scalar.activation(prod[:, m, :], prod[:, m, :], ACT.Identity, accum_out=dots[:, m:m + 1])
                nc.scalar.activation(unused[:, n, :], wn[:, m, :], ACT.Abs, accum_out=bound[:, m:m + 1]) \
                    .then_inc(w_summed, 1)
            for kc in range(KC):
                sum_pass(0, 0, 0, kc)
            for n in range(2):
                w_parts_hi(n)
            for kc in range(KC):
                sum_pass(0, 0, 1, kc)
            for n in range(2, 12):
                w_parts_hi(n)
            for kc in range(KC):
                normalised_hi(0, 0, kc)
            for F, item in enumerate(HEAD_START):
                filler_hi(F, item, 0, 0)
                if F == 5:
                    for n in range(12, 16):
                        w_parts_hi(n)
            numerators(0, 0)

            def batch(b, par, first, last):
                slots = slots_of(b, first, last)
                for i in range(STEPS):
                    if i % 4 == 2 and not (first and i < 4):
                        outputs_read(b * 16 + (i // 4 - 1), (i // 4 - 1) % 16 // 4)
                    for half in range(2):
                        c = slice(4 * half, 4 * half + 4)
                        act.wait_ge(t_done, b * (2 * STEPS) + (2 * i + 1 + half))
                        nc.scalar.activation(PT[:, i % 2, HI, c], TP[:, c], ACT.Copy, scale=PS) \
                            .then_inc(ph_done, 1)
                    if i + 1 < STEPS:
                        numerators(b, i + 1)
                    elif not last:
                        numerators(b + 1, 0)
                    if i % 2 == 1 and i // 2 in slots:
                        item, off = slots[i // 2]
                        filler_hi(filler_number(b, i // 2), item, b + off, (par + off) % 2)
                    if not last:
                        for kc in range(KC):
                            if i == SUM_STEPS[kc]:
                                sum_pass(b + 1, 1 - par, 0, kc)
                            if i == SQUARE_STEPS[kc]:
                                sum_pass(b + 1, 1 - par, 1, kc)
                            if i == PARTS_STEPS[kc]:
                                normalised_hi(b + 1, 1 - par, kc)

            run_batches(act, batch)
            outputs_read(16 * B - 1, 3)

        @block.vector
        def _(dve):
            v = nc.vector
            chain = Chain(dve, dve_chain)
            chain.per_batch = DVE_CHAIN
            dve.wait_ge(gn_loaded, 32)
            for n, m in enumerate(W_ORDER):
                if n % 4 == 0:
                    dve.wait_ge(w_loaded[m // 4], 32)
                v.tensor_tensor(prod[:, m, :], wn[:, m, :], gb, ALU.mult)
                v.tensor_tensor(wn[:, m, :], wn[:, m, :], gw, ALU.mult).then_inc(w_times_gn, 1)
            dve.wait_ge(w_summed, 12)
            dve.wait_ge(bias_loaded, 7 * 16)
            chain(v.tensor_tensor(bq[:], bq[:], dots[:], ALU.add))
            chain(v.tensor_scalar(tmp[:], bq[:], -1.0, None, ALU.mult))
            chain(v.tensor_tensor(tmp[:], tmp[:], bq[:], ALU.max))
            chain(v.scalar_tensor_tensor(bound[:], bound[:], XS, tmp[:], ALU.mult, ALU.add))
            chain(v.tensor_scalar(bound[:], bound[:], 1e-30, None, ALU.max))
            chain(v.reciprocal(omega[:], bound[:]))
            chain(v.tensor_scalar(omega[:], omega[:], ROW * XS, None, ALU.mult))

            def w_rows_scaled(n):
                m = W_ORDER[n]
                v.tensor_scalar(wn[:, m, :], wn[:, m, :], omega[:, m:m + 1], None, ALU.mult) \
                    .then_inc(w_scaled, 1)

            def w_parts_lo(n):
                dve.wait_ge(w_hi, n + 1)
                m = W_ORDER[n] if n < 12 else n - 12
                W = Wqkv if n < 12 else Wp
                cols = slice(m * P, (m + 1) * P)
                v.tensor_tensor(W[:, LO, :, cols], wbank[:, n % 4], W[:, HI, :, cols], ALU.subtract) \
                    .then_inc(w_lo, 1)

            def result_scales():
                dve.wait_ge(tops, 2)
                chain(v.tensor_tensor(sscale[:], gtop[:, 0:1], gtop[:, 1:2], ALU.mult))
                chain(v.tensor_scalar(sscale[:], sscale[:], float(D) ** -0.5 / TOP ** 2, None, ALU.mult))
                chain(v.reciprocal(top2[:], gtop[:]))
                chain(v.tensor_scalar(top2[:], top2[:], TOP, None, ALU.mult))
                for k in range(2):
                    m = slice(4 * k, 4 * k + 4)
                    chain(v.tensor_scalar(cq[:, m], bound[:, m], top2[:, k:k + 1], 1.0 / (XS * ROW * XS),
                                          ALU.mult, ALU.mult))
                    chain(v.tensor_scalar(bq[:, m], bq[:, m], top2[:, k:k + 1], None, ALU.mult))
                chain(v.tensor_scalar(tmp[:, 8:12], omega[:, 8:12], TOP / (ROW * XS), None, ALU.mult))
                chain(v.tensor_tensor(bq[:, 8:12], bq[:, 8:12], tmp[:, 8:12], ALU.mult))

            def v_bound_diagonals():
                v.memset(ones, 1.0)
                for p in range(PAIRS):
                    last = v.tensor_scalar(diag[:, p, :], id32[:], bound[:, 8 + p:9 + p], None, ALU.mult)
                last.then_inc(v_bounds, 1)

            def proj_times_bounds():
                dve.wait_ge(wp_loaded, 16)
                dve.wait_ge(v_bounds_wide, 1)
                brow = AV[:].rearrange("p a t -> p (a t)").unsqueeze(1).to_broadcast([P, 4, C])
                chain(v.tensor_tensor(wpn, wpn, brow, ALU.mult))

            def proj_sums():
                chain(v.tensor_reduce(cp[:], wpn, AX.X, ALU.add, apply_absolute_value=True))
                chain(v.tensor_scalar(cp[:], cp[:], 1e-30, None, ALU.max))
                chain(v.reciprocal(tmp[:, 0:4], cp[:]))
                chain(v.tensor_scalar(tmp[:, 0:4], tmp[:, 0:4], ROW, None, ALU.mult))
                chain(v.tensor_scalar(cp[:], cp[:], 1.0 / (ROW * TOP), None, ALU.mult))

            def proj_rows_scaled():
                v.tensor_tensor(wpn, wpn, tmp[:, 0:4].unsqueeze(2).to_broadcast([P, 4, C]), ALU.mult) \
                    .then_inc(wp_scaled, 1)

            def group_mean(X):
                dve.wait_ge(stat_out, X * 2 + 1)
                wait(dve, xy_done, X * 4)
                v.tensor_scalar(ngm[:], AV[:, 1, 0:KC], -1.0, None, ALU.mult).then_inc(stat_read, 1)

            def group_variance(X):
                dve.wait_ge(stat_out, X * 2 + 2)
                v.tensor_scalar(na[:], AV[:, 1, 0:KC], EPS, None, ALU.add).then_inc(stat_read, 1)
                dve.wait_ge(stat_read, X * 2 + 2)
                v.tensor_scalar(hv[:], na[:], -0.5, None, ALU.mult)
                chain(v.tensor_scalar(ny[:].bitcast(U32), na[:].bitcast(U32), 1, None,
                                      ALU.logical_shift_right))
                v.tensor_scalar(ny[:].bitcast(U32), ny[:].bitcast(U32), -1.0, 1597463007.0,
                                ALU.mult, ALU.add).then_inc(guessed, 1)

            def scaled_filler(F, item, bank=FB[:]):
                kind, i0, i1 = item
                dve.wait_ge(filler_psum, F + 1)
                wait(dve, filler_out, F)
                if kind == "v":
                    ins = v.tensor_scalar(yf[:], bank, TOP / (XS * ROW * XS), None, ALU.mult)
                elif kind == "qk":
                    m = (i1 // 2) * 4 + i0
                    ins = v.tensor_scalar(yf[:], bank, cq[:, m:m + 1], bq[:, m:m + 1], ALU.mult, ALU.add)
                else:
                    ins = v.tensor_scalar(yf[:], bank, cp[:, i1:i1 + 1], bp[:, i1:i1 + 1], ALU.mult, ALU.add)
                ins.then_inc(y_done, 1)

            def row_max(b, i):
                dve.wait_ge(s_done, b * STEPS + (i + 1))
                q = i % 4
                chain(v.tensor_reduce(nmax[:, q:q + 1], SC[:, i % 2, :], AX.X, ALU.max, negate=True))
                v.tensor_scalar(nbias[:, q:q + 1], nmax[:, q:q + 1], sscale[:, 0:1], None, ALU.mult) \
                    .then_inc(nb_done, 1)

            def normalised_outputs(count, gpar):
                dve.wait_ge(av_done, count + 1)
                dve.wait_ge(ri_done, count + 1)
                wait(dve, ot_done, count)
                v.scalar_tensor_tensor(on[:], AV[:, 0, :].rearrange("p (k d) -> p k d", d=D), 1.0 / PS,
                                       rinv[:, gpar, :].unsqueeze(2).to_broadcast([P, 4, D]),
                                       ALU.mult, ALU.mult).then_inc(on_done, 1)

            def normalised(X, kc):
                dve.wait_ge(norm_ready, X + 1)
                v.tensor_scalar(xc[:, kc, :], xc[:, kc, :], ngm[:, kc:kc + 1], rs[:, kc:kc + 1],
                                ALU.add, ALU.mult).then_inc(xy_done, 1)

            def reciprocals(count, gpar):
                dve.wait_ge(e_done, (count + 1) * 4)
                v.reciprocal(rinv[:, gpar, :], acc[:, gpar, :]).then_inc(ri_done, 1)

            for n in range(6):
                w_rows_scaled(n)
            group_mean(0)
            for n in range(6, 12):
                w_rows_scaled(n)
            v.tensor_reduce(top2[:], bound[:, 0:8].rearrange("p (k m) -> p k m", k=2), AX.X, ALU.max) \
                .then_inc(tops, 1)
            for n in range(2):
                w_parts_lo(n)
            group_variance(0)
            for n in range(2, 12):
                w_parts_lo(n)

            def first_normalised_lo(kc):
                dve.wait_ge(xh_done, kc + 1)
                v.tensor_tensor(XN[:, 0, LO, kc, :], xc[:, kc, :], XN[:, 0, HI, kc, :], ALU.subtract) \
                    .then_inc(xn_done, 1)

            normalised(0, 0)
            normalised(0, 1)
            first_normalised_lo(0)
            normalised(0, 2)
            first_normalised_lo(1)
            normalised(0, 3)
            first_normalised_lo(2)
            first_normalised_lo(3)
            result_scales()
            v_bound_diagonals()
            between = {1: proj_times_bounds, 2: proj_sums, 3: proj_rows_scaled}
            for F, item in enumerate(HEAD_START):
                scaled_filler(F, item, TPB if F % 2 else FB[:])
                if F in between:
                    between[F]()
                if F == 5:
                    for n in range(12, 16):
                        w_parts_lo(n)
            row_max(0, 0)

            def batch(b, par, first, last):
                slots = slots_of(b, first, last)
                for i in range(STEPS):
                    g, k = i // 4, i % 4
                    if k == 1 and not (first and g < 1):
                        normalised_outputs(b * 16 + (g - 1), (g - 1) % 2)
                    if i - 1 == MEAN_STEP and not last:
                        group_mean(b + 1)
                    if i - 1 == VAR_STEP and not last:
                        group_variance(b + 1)
                    if i + 1 < STEPS:
                        row_max(b, i + 1)
                    elif not last:
                        row_max(b + 1, 0)
                    if i % 2 == 1 and i // 2 in slots:
                        scaled_filler(filler_number(b, i // 2), slots[i // 2][0])
                    if k == 0 and not (first and g < 1):
                        reciprocals(b * 16 + (g - 1), (g - 1) % 2)
                    for half in range(2):
                        c = slice(4 * half, 4 * half + 4)
                        dve.wait_ge(ph_done, b * (2 * STEPS) + (2 * i + 1 + half))
                        v.scalar_tensor_tensor(PT[:, i % 2, LO, c], TP[:, c], PS, PT[:, i % 2, HI, c],
                                               ALU.mult, ALU.subtract).then_inc(pl_done, 1)
                    for kc in range(KC):
                        if i == NORM_STEPS[kc] and not last:
                            normalised(b + 1, kc)

            run_batches(dve, batch, chain)
            reciprocals(16 * B - 1, 1)
            normalised_outputs(16 * B - 1, 1)
            for s in range(8):
                scaled_filler(filler_number(B - 1, AHEAD + s), SLOTS[s], TPB if s % 2 else FB[:])

        @block.gpsimd
        def _(pool):
            v = nc.gpsimd
            chain = Chain(pool, pool_chain)
            chain.per_batch = POOL_CHAIN
            chain(v.memset(id32[:], 0.0))
            v.affine_select(out=id32[:], in_=id32[:], compare_op=ALU.not_equal, fill=1.0, base=0,
                            pattern=[[-1, P]], channel_multiplier=1).then_inc(consts, 1)
            chain(v.memset(gavg[:], 1.0 / (CPG * T)))
            gv = gavg[:].rearrange("p (g c) -> p g c", c=CPG)
            chain(v.affine_select(out=gv, in_=gv, compare_op=ALU.is_ge, fill=0.0, base=0,
                                  pattern=[[-CPG, P // CPG], [0, CPG]], channel_multiplier=1))
            v.affine_select(out=gv, in_=gv, compare_op=ALU.is_ge, fill=0.0, base=CPG - 1,
                            pattern=[[CPG, P // CPG], [0, CPG]], channel_multiplier=-1).then_inc(consts, 1)
            chain.alone = True
            pool.wait_ge(tops, 1)
            v.partition_all_reduce(gtop[:], top2[:], P, RMAX).then_inc(tops, 1)

            def inverse_std(X):
                apart(pool, X + 1, X * 4)
                pool.wait_ge(guessed, X + 1)
                wait(pool, xy_done, X * 4)
                for _ in range(3):
                    chain.alone = False
                    chain(v.tensor_tensor(na[:], ny[:], ny[:], ALU.mult))
                    chain.alone = True
                    chain(v.tensor_tensor(na[:], na[:], hv[:], ALU.mult))
                    chain.alone = False
                    chain(v.tensor_scalar(na[:], na[:], 1.5, None, ALU.add))
                    chain.alone = True
                    chain(v.tensor_tensor(ny[:], na[:], ny[:], ALU.mult))
                v.tensor_scalar(rs[:], ny[:], XS, None, ALU.mult).then_inc(norm_ready, 1)

            def normalised_lo(X, par, kc):
                pool.wait_ge(xh_done, X * 4 + (kc + 1))
                v.tensor_tensor(XN[:, par, LO, kc, :], xc[:, kc, :], XN[:, par, HI, kc, :],
                                ALU.subtract).then_inc(xn_done, 1)

            def use_filler(F, item, b, par, parts):
                kind, i0, i1 = item
                if kind == "proj":
                    i = 4 * i0 + i1
                    pool.wait_ge(y_done, F + 1)
                    pool.wait_ge(res_loaded[i], b * 16 + 16)
                    ins = v.tensor_tensor(xres[:, i, :], xres[:, i, :], yf[:], ALU.add)
                else:
                    hi, lo = ((V[:, par, HI, i0, :], V[:, par, LO, i0, :]) if kind == "v" else
                              (nat[:, i1 % 2, HI, :], nat[:, i1 % 2, LO, :]))
                    pool.wait_ge(yh_done, parts)
                    ins = v.tensor_tensor(lo, yf[:], hi, ALU.subtract)
                ins.then_inc(filler_out, 1)

            def outputs_parts(count, g, be):
                pair, u = g // 4, g % 4
                cols = slice(u * TG, (u + 1) * TG)
                used = be * 32 + (12 + 4 * (u // 2))
                apart(pool, count + 1, used)
                pool.wait_ge(at_read, count + 1)
                if not (isinstance(be, int) and be == 0):
                    pool.wait_ge(filler_psum, used)
                chain(v.tensor_copy(AT[:, HI, pair, cols], at[:]))
                v.tensor_tensor(AT[:, LO, pair, cols], at[:], AT[:, HI, pair, cols], ALU.subtract) \
                    .then_inc(at_done, 1)

            inverse_std(0)
            for F, item in enumerate(HEAD_START):
                use_filler(F, item, 0, 0, F + 1)

            def batch(b, par, first, last):
                slots = slots_of(b, first, last)
                for i in range(STEPS):
                    g, k = i // 4, i % 4
                    if i % 2 == 1 and i // 2 in slots:
                        item, off = slots[i // 2]
                        use_filler(filler_number(b, i // 2), item, b + off, (par + off) % 2,
                                   13 + i // 2 if first and i < 8 else b * 24 + (i // 2 + 9))
                    if k == 0 and not (first and g < 2):
                        outputs_parts(b * 16 + (g - 2), (g - 2) % 16, b if g >= 2 else b - 1)
                    if not last:
                        if i == RSQRT_STEP:
                            inverse_std(b + 1)
                        for kc in range(KC):
                            if i == PARTS_STEPS[kc]:
                                normalised_lo(b + 1, 1 - par, kc)

            run_batches(pool, batch, chain)
            for g in (14, 15):
                outputs_parts(16 * (B - 1) + g, g, B - 1)
            for s in range(8):
                use_filler(filler_number(B - 1, AHEAD + s), SLOTS[s], B - 1, 1, None)


DVE_CHAIN = 65
POOL_CHAIN = 28

_INS = ["x", "L0_conv_gn_w", "L0_conv_gn_b", "L0_conv_qkv_w", "L0_conv_qkv_b", "L0_conv_proj_w", "L0_conv_proj_b"]


def kernel(**inputs):
    import numpy as _np
    import concourse.bacc as _bacc
    from concourse import mybir as _mybir
    from concourse.bass_utils import run_bass_kernel_spmd as _run

    nc = _bacc.Bacc("TRN2", target_bir_lowering=False, num_devices=1)
    arrays, args = {}, []
    for name in _INS:
        a = _np.ascontiguousarray(inputs[name])
        arrays[f"in_{name}_dram"] = a
        args.append(nc.dram_tensor(f"in_{name}_dram", a.shape, _mybir.dt.from_np(a.dtype), kind="ExternalInput").ap())
    shape = inputs["x"].shape
    args.append(nc.dram_tensor("out_dram", shape, _mybir.dt.from_np(_np.dtype("float32")), kind="ExternalOutput").ap())
    bass_groupnorm_attention_kernel(nc, *args)
    r = _run(nc, [arrays], core_ids=[0])
    return r.results[0]["out_dram"]
```
